# Optimizing a Trainium2 kernel written in Bass

```python
import numpy as np
import jax
import jax.numpy as jnp

def _softmax(x, axis=-1):
    return jax.nn.softmax(x, axis=axis)

def _gelu(x):
    return jax.nn.gelu(x, approximate=True)

def _silu(x):
    return jax.nn.silu(x)

def _sigmoid(x):
    return jax.nn.sigmoid(x)

def _layernorm(x, axis=-1, eps=1e-05):
    m = jnp.mean(x, axis=axis, keepdims=True)
    v = jnp.var(x, axis=axis, keepdims=True)
    return (x - m) / jnp.sqrt(v + eps)

def _scatter_add(tgt, idx, src, axis=0):
    return tgt.at[idx].add(src)

def _segment_sum(src, seg, n):
    return jax.ops.segment_sum(src, seg, n)
kernel_name = 'mk_recurrent_d1_jaxref_r4_a17ca3'

def setup_inputs(seed: int=0):
    np.random.seed(seed)
    _w = jnp.asarray

    def _L0_attn_setup():
        import math
        import jax, jax.numpy as jnp
        import numpy as np
        E = 256
        H = 16
        KVH = 8
        N_REP = H // KVH
        HD = E // H // 2
        DEPTH = 12
        LAMBDA_INIT = 0.8 - 0.6 * math.exp(-0.3 * DEPTH)
        EPS = 1e-06
        ROPE_BASE = 10000.0

        def rope_tables(T):
            inv_freq = 1.0 / ROPE_BASE ** (np.arange(0, HD, 2, dtype=np.float32) / HD)
            t = np.arange(T, dtype=np.float32)
            freqs = np.outer(t, inv_freq)
            return (jnp.asarray(np.cos(freqs)), jnp.asarray(np.sin(freqs)))

        def apply_rope(x, cos, sin):
            d = x.shape[-1] // 2
            c = cos[None, :, None, :]
            s = sin[None, :, None, :]
            x1, x2 = (x[..., :d], x[..., d:])
            return jnp.concatenate([x1 * c + x2 * s, -x1 * s + x2 * c], axis=-1)

        def causal_attn(q, k, v, scale):
            T = q.shape[1]
            mask = jnp.tril(jnp.ones((T, T), dtype=bool))
            s = jnp.einsum('bthd,bshd->bhts', q, k) * scale
            s = jnp.where(mask[None, None], s, jnp.finfo(s.dtype).min)
            p = jax.nn.softmax(s, axis=-1)
            return jnp.einsum('bhts,bshd->bthd', p, v)
        key = jax.random.key(seed)
        ks = jax.random.split(key, 10)
        s = 0.02
        return {'x': jax.random.normal(ks[0], (4, 256, E), jnp.float32), 'Wq': jax.random.normal(ks[1], (E, E), jnp.float32) * s, 'Wk': jax.random.normal(ks[2], (E, E // N_REP), jnp.float32) * s, 'Wv': jax.random.normal(ks[3], (E, E // N_REP), jnp.float32) * s, 'Wo': jax.random.normal(ks[4], (E, E), jnp.float32) * s, 'lambda_q1': jax.random.normal(ks[5], (HD,), jnp.float32) * 0.1, 'lambda_k1': jax.random.normal(ks[6], (HD,), jnp.float32) * 0.1, 'lambda_q2': jax.random.normal(ks[7], (HD,), jnp.float32) * 0.1, 'lambda_k2': jax.random.normal(ks[8], (HD,), jnp.float32) * 0.1, 'rms_w': jnp.ones((2 * HD,), jnp.float32)}
    _L0_attn_in = _L0_attn_setup()

    def _L0_ffn_setup():
        import jax, jax.numpy as jnp
        import numpy as np
        H, I, E, NS, C = (256, 256, 6, 2, 2)
        TOPK = 2
        TEMP = 1.0
        EPS = 1e-06
        key = jax.random.key(seed)
        ks = jax.random.split(key, 20)
        sd = 0.02
        inp = {'x': jax.random.normal(ks[0], (4, 512, H), jnp.float32), 'router_W': jax.random.normal(ks[1], (C, H, E), jnp.float32) * sd, 'router_b': jax.random.normal(ks[2], (C, E), jnp.float32) * sd, 'gate_bias': jax.random.normal(ks[3], (C, E), jnp.float32) * sd, 'exp_Wup': jax.random.normal(ks[4], (E, H, I), jnp.float32) * sd, 'exp_bup': jnp.zeros((E, I), jnp.float32), 'exp_Wg': jax.random.normal(ks[5], (E, I, I), jnp.float32) * sd, 'exp_bg': jnp.zeros((E, I), jnp.float32), 'exp_Wdown': jax.random.normal(ks[6], (E, I, H), jnp.float32) * sd, 'exp_bdown': jnp.zeros((E, H), jnp.float32), 'share_Wup': jax.random.normal(ks[7], (H, NS * I), jnp.float32) * sd, 'share_bup': jnp.zeros((NS * I,), jnp.float32), 'share_Wg': jax.random.normal(ks[8], (I, I), jnp.float32) * sd, 'share_bg': jnp.zeros((I,), jnp.float32), 'share_Wdown': jax.random.normal(ks[9], (I, H), jnp.float32) * sd, 'share_bdown': jnp.zeros((H,), jnp.float32), 'norm_w': jnp.ones((C, H), jnp.float32)}
        return inp
    _L0_ffn_in = _L0_ffn_setup()
    _d = {'L0_attn_x': _L0_attn_in['x'], 'L0_attn_Wq': _L0_attn_in['Wq'], 'L0_attn_Wk': _L0_attn_in['Wk'], 'L0_attn_Wv': _L0_attn_in['Wv'], 'L0_attn_Wo': _L0_attn_in['Wo'], 'L0_attn_lambda_q1': _L0_attn_in['lambda_q1'], 'L0_attn_lambda_k1': _L0_attn_in['lambda_k1'], 'L0_attn_lambda_q2': _L0_attn_in['lambda_q2'], 'L0_attn_lambda_k2': _L0_attn_in['lambda_k2'], 'L0_attn_rms_w': _L0_attn_in['rms_w'], 'L0_ffn_router_W': _L0_ffn_in['router_W'], 'L0_ffn_router_b': _L0_ffn_in['router_b'], 'L0_ffn_gate_bias': _L0_ffn_in['gate_bias'], 'L0_ffn_exp_Wup': _L0_ffn_in['exp_Wup'], 'L0_ffn_exp_bup': _L0_ffn_in['exp_bup'], 'L0_ffn_exp_Wg': _L0_ffn_in['exp_Wg'], 'L0_ffn_exp_bg': _L0_ffn_in['exp_bg'], 'L0_ffn_exp_Wdown': _L0_ffn_in['exp_Wdown'], 'L0_ffn_exp_bdown': _L0_ffn_in['exp_bdown'], 'L0_ffn_share_Wup': _L0_ffn_in['share_Wup'], 'L0_ffn_share_bup': _L0_ffn_in['share_bup'], 'L0_ffn_share_Wg': _L0_ffn_in['share_Wg'], 'L0_ffn_share_bg': _L0_ffn_in['share_bg'], 'L0_ffn_share_Wdown': _L0_ffn_in['share_Wdown'], 'L0_ffn_share_bdown': _L0_ffn_in['share_bdown'], 'L0_ffn_norm_w': _L0_ffn_in['norm_w']}
    _x0 = _d['L0_attn_x']
    _d['L0_attn_x'] = jax.random.normal(jax.random.fold_in(jax.random.key(seed), 1), (4, 1024, 256), dtype=_x0.dtype)
    del _x0
    return _d

def reference(L0_attn_x, L0_attn_Wq, L0_attn_Wk, L0_attn_Wv, L0_attn_Wo, L0_attn_lambda_q1, L0_attn_lambda_k1, L0_attn_lambda_q2, L0_attn_lambda_k2, L0_attn_rms_w, L0_ffn_router_W, L0_ffn_router_b, L0_ffn_gate_bias, L0_ffn_exp_Wup, L0_ffn_exp_bup, L0_ffn_exp_Wg, L0_ffn_exp_bg, L0_ffn_exp_Wdown, L0_ffn_exp_bdown, L0_ffn_share_Wup, L0_ffn_share_bup, L0_ffn_share_Wg, L0_ffn_share_bg, L0_ffn_share_Wdown, L0_ffn_share_bdown, L0_ffn_norm_w):

    def _L0_attn_ref(x, Wq, Wk, Wv, Wo, lambda_q1, lambda_k1, lambda_q2, lambda_k2, rms_w):
        import math
        import jax, jax.numpy as jnp
        import numpy as np
        E = 256
        H = 16
        KVH = 8
        N_REP = H // KVH
        HD = E // H // 2
        DEPTH = 12
        LAMBDA_INIT = 0.8 - 0.6 * math.exp(-0.3 * DEPTH)
        EPS = 1e-06
        ROPE_BASE = 10000.0

        def rope_tables(T):
            inv_freq = 1.0 / ROPE_BASE ** (np.arange(0, HD, 2, dtype=np.float32) / HD)
            t = np.arange(T, dtype=np.float32)
            freqs = np.outer(t, inv_freq)
            return (jnp.asarray(np.cos(freqs)), jnp.asarray(np.sin(freqs)))

        def apply_rope(x, cos, sin):
            d = x.shape[-1] // 2
            c = cos[None, :, None, :]
            s = sin[None, :, None, :]
            x1, x2 = (x[..., :d], x[..., d:])
            return jnp.concatenate([x1 * c + x2 * s, -x1 * s + x2 * c], axis=-1)

        def causal_attn(q, k, v, scale):
            T = q.shape[1]
            mask = jnp.tril(jnp.ones((T, T), dtype=bool))
            s = jnp.einsum('bthd,bshd->bhts', q, k) * scale
            s = jnp.where(mask[None, None], s, jnp.finfo(s.dtype).min)
            p = jax.nn.softmax(s, axis=-1)
            return jnp.einsum('bhts,bshd->bthd', p, v)
        B, T, _ = x.shape
        q = (x @ Wq).reshape(B, T, 2 * H, HD)
        k = (x @ Wk).reshape(B, T, 2 * KVH, HD)
        v = (x @ Wv).reshape(B, T, KVH, 2, HD)
        cos, sin = rope_tables(T)
        q = apply_rope(q, cos, sin)
        k = apply_rope(k, cos, sin)
        q = q.reshape(B, T, H, 2, HD)
        k = k.reshape(B, T, KVH, 2, HD)
        q1, q2 = (q[:, :, :, 0], q[:, :, :, 1])
        k1, k2 = (k[:, :, :, 0], k[:, :, :, 1])
        vcat = v.reshape(B, T, KVH, 2 * HD)
        k1 = jnp.repeat(k1, N_REP, axis=2)
        k2 = jnp.repeat(k2, N_REP, axis=2)
        vcat = jnp.repeat(vcat, N_REP, axis=2)
        scale = HD ** (-0.5)
        attn1 = causal_attn(q1, k1, vcat, scale)
        attn2 = causal_attn(q2, k2, vcat, scale)
        lambda_1 = jnp.exp(jnp.sum(lambda_q1 * lambda_k1))
        lambda_2 = jnp.exp(jnp.sum(lambda_q2 * lambda_k2))
        lambda_full = lambda_1 - lambda_2 + LAMBDA_INIT
        attn = attn1 - lambda_full * attn2
        rms = jnp.sqrt(jnp.mean(attn * attn, axis=-1, keepdims=True) + EPS)
        attn = attn / rms * rms_w
        attn = attn * (1.0 - LAMBDA_INIT)
        attn = attn.reshape(B, T, H * 2 * HD)
        return attn @ Wo

    def _L0_ffn_ref(x, router_W, router_b, gate_bias, exp_Wup, exp_bup, exp_Wg, exp_bg, exp_Wdown, exp_bdown, share_Wup, share_bup, share_Wg, share_bg, share_Wdown, share_bdown, norm_w):
        import jax, jax.numpy as jnp
        import numpy as np
        H, I, E, NS, C = (256, 256, 6, 2, 2)
        TOPK = 2
        TEMP = 1.0
        EPS = 1e-06
        B, S, Hd = x.shape
        xf = x.reshape(-1, Hd)
        for j in range(C):
            residual = xf
            gate = (xf @ router_W[j] + router_b[j]) / TEMP
            biased = gate + gate_bias[j]
            _, ids = jax.lax.top_k(biased, TOPK)
            sel = (ids[:, :, None] == jnp.arange(E)[None, None, :]).any(axis=1)
            weights = jax.nn.softmax(jnp.where(sel, gate, -jnp.inf), axis=-1)
            h = jnp.einsum('nh,ehi->eni', xf, exp_Wup) + exp_bup[:, None, :]
            h = jax.nn.silu(jnp.einsum('eni,eij->enj', h, exp_Wg) + exp_bg[:, None, :]) * h
            eo = jnp.einsum('eni,eih->enh', h, exp_Wdown) + exp_bdown[:, None, :]
            combined = jnp.einsum('ne,enh->nh', weights, eo)
            s = (xf @ share_Wup + share_bup).reshape(-1, NS, I)
            s = jax.nn.silu(s @ share_Wg + share_bg) * s
            share_out = (s @ share_Wdown + share_bdown).sum(axis=1)
            z = combined + share_out
            y = residual + z
            y = y * jax.lax.rsqrt(jnp.mean(y * y, axis=-1, keepdims=True) + EPS) * norm_w[j]
            xf = y
        return xf.reshape(B, S, Hd)
    x = L0_attn_x
    xn = _layernorm(x, axis=-1)
    s = _L0_attn_ref(xn, L0_attn_Wq, L0_attn_Wk, L0_attn_Wv, L0_attn_Wo, L0_attn_lambda_q1, L0_attn_lambda_k1, L0_attn_lambda_q2, L0_attn_lambda_k2, L0_attn_rms_w)
    g = _silu(_L0_ffn_ref(xn, L0_ffn_router_W, L0_ffn_router_b, L0_ffn_gate_bias, L0_ffn_exp_Wup, L0_ffn_exp_bup, L0_ffn_exp_Wg, L0_ffn_exp_bg, L0_ffn_exp_Wdown, L0_ffn_exp_bdown, L0_ffn_share_Wup, L0_ffn_share_bup, L0_ffn_share_Wg, L0_ffn_share_bg, L0_ffn_share_Wdown, L0_ffn_share_bdown, L0_ffn_norm_w))
    x = x + s * g
    return x

_drawn_inputs = setup_inputs


def setup_inputs(seed=0):
    import zlib

    import numpy as np

    out = dict(_drawn_inputs(seed))
    spreads = {'L0_attn_rms_w': (1.0, 0.6),
     'L0_ffn_exp_bup': (0.0, 0.8),
     'L0_ffn_exp_bg': (0.0, 2.0),
     'L0_ffn_exp_bdown': (0.0, 2.0),
     'L0_ffn_share_bup': (0.0, 0.8),
     'L0_ffn_share_bg': (0.0, 2.0),
     'L0_ffn_share_bdown': (0.0, 2.0),
     'L0_ffn_norm_w': (1.0, 0.6)}
    factors = {'L0_attn_lambda_q1': 200.0,
     'L0_attn_lambda_k1': 8.0,
     'L0_attn_lambda_q2': 64.0,
     'L0_attn_lambda_k2': 64.0,
     'L0_ffn_router_W': 8.0,
     'L0_ffn_router_b': 47.909,
     'L0_ffn_gate_bias': 56.613,
     'L0_ffn_exp_Wup': 8.0,
     'L0_ffn_exp_Wg': 8.0,
     'L0_ffn_exp_Wdown': 8.0,
     'L0_ffn_share_Wup': 8.0,
     'L0_ffn_share_Wg': 8.0,
     'L0_ffn_share_Wdown': 8.0,
     'L0_attn_Wq': 4.534,
     'L0_attn_Wk': 4.369}
    for name, (base, spread) in spreads.items():
        noise = np.random.default_rng([zlib.crc32(name.encode()), seed]).standard_normal(out[name].shape)
        drawn = base * np.exp(spread * noise) if base else spread * noise
        out[name] = jnp.asarray(drawn.astype(out[name].dtype))
    for name, factor in factors.items():
        out[name] = (out[name] * factor).astype(out[name].dtype)
    return out
```

```python
from contextlib import ExitStack
import math

import numpy as np

import concourse.bass as bass
from concourse import mybir

F32 = mybir.dt.float32
F32R = mybir.dt.float32r
BF16 = mybir.dt.bfloat16
ALU = mybir.AluOpType
ACT = mybir.ActivationFunctionType
AX = mybir.AxisListType.X

P = 128
B, T, E = 4, 1024, 256
N = B * T
KT = E // P
C = 512
TB = C // P
NCH = N // C
NQ, NK, KVH, HD = 32, 16, 8, 8
VD = 2 * HD
MAPS = NQ // KVH
UNITS = B * KVH
NEXP, NSH, LAYERS = 6, 2, 2
NE = NEXP + NSH
A_STEPS, B_STEPS, C_STEPS, D_STEPS = 38, 10, 66, 6
LAMBDA_INIT = 0.8 - 0.6 * math.exp(-0.3 * 12)
SCALE = HD ** -0.5
NEG = -1e30
SQ_MAX = 2.0 ** 64

ZROWS = 96
SROWS = ZROWS + 2

GROUPS = [(h, j) for h in range(2) for j in range(4 * (h + 1))]
JOBS = MAPS * len(GROUPS)
MAXP = [(i, 0, mp) for i in range(4) for mp in range(2)] + \
       [(i, p, mp) for i in range(4, 8) for p in range(2) for mp in range(2)]
MAXA = 8
LEAD = 42
PRING = 8
SHIFT_B_AT, OT_B_AT, OT_A_AT, SHIFT_A_AT = 9, 12, 24, 27
OT_EVAC_B_AT, OT_EVAC_A_AT = 2, 18
VALUES_AT = 1

W_UP, W_GATE, W_DOWN, NW = 0, NE, NE + NEXP + 1, NE + 2 * (NEXP + 1)


class Steps:

    def __init__(self, eng, sem):
        self.eng, self.sem, self.base, self.n = eng, sem, 0, 0

    def done(self, ins):
        self.n += 1
        ins.then_inc(self.sem, 1)

    def wait(self):
        self.eng.wait_ge(self.sem, self.base + self.n)

    def enter(self, turn, per):
        self.start = self.base + self.n
        self.base, self.n, self.per = self.start + turn * per, 0, per

    def leave(self, turns):
        assert self.n == self.per, (self.n, self.per)
        self.base, self.n = self.start + turns * self.per, 0


def build(nc, t, out):
    with ExitStack() as ctx:
        def sb(name, shape, dt=F32):
            return ctx.enter_context(nc.sbuf_tensor(name, shape, dt))

        def sem(name):
            return ctx.enter_context(nc.semaphore(name))

        def dram(name, shape, dt=F32):
            return nc.dram_tensor(name, shape, dt).ap()

        q_scr = dram("q_scr", (2, HD, UNITS, MAPS, T), F32R)
        k_scr = dram("k_scr", (HD, 2, UNITS, 2, T), F32R)
        v_scr = dram("v_scr", (B, KVH, T, VD))
        x_scr = dram("x_scr", (NCH, P, KT, C))
        a_scr = dram("a_scr", (UNITS, 2 * TB, P, 2 * VD))

        WH = sb("WH", [P, NW, 512], F32R)
        WL = sb("WL", [P, NW, 512], F32R)
        wstage = sb("wstage", [P, 2, 512])
        wq = sb("wq", [P, KT, 2, P])
        wk = sb("wk", [P, KT, 2, P])
        wv = sb("wv", [P, KT, P])
        wo = sb("wo", [P, KT, E])
        ident = sb("ident", [P, P])
        identb = sb("identb", [P, P], BF16)
        maskq = sb("maskq", [P, P], BF16)
        maskk = sb("maskk", [P, P], BF16)
        meanw = sb("meanw", [P, P])
        small = sb("small", [P, 512])
        rbuf = sb("rbuf", [P, 12288], F32R)
        fbuf = sb("fbuf", [P, 8704])
        wT = sb("wT", [32, 2, C], F32R)
        whl = sb("whl", [32, 16, 32], F32R)
        selw = sb("selw", [32, NEXP, P], F32R)
        bdr = sb("bdr", [32, 2, E], F32R)

        def carve(buf, sizes):
            views, at = [], 0
            for shape in sizes:
                n = int(np.prod(shape))
                v = buf[:, at:at + n]
                at += n
                names = "abcd"[:len(shape)]
                if len(shape) > 1:
                    v = v.rearrange(f"p ({' '.join(names)}) -> p {' '.join(names)}",
                                    **dict(zip(names, shape)))
                views.append(v)
            assert at <= buf.shape[1], (at, buf.shape)
            return views

        (lamv, lamp, lams, lame, lamneg, sgn, bup, bg, bds, nw, rmsw, mv, bst, rst, epsn) = carve(small, [
            (4, HD), (2, HD), (2,), (2,), (1,), (1,), (NE, KT), (NEXP + 1, KT), (KT,), (LAYERS, KT), (1,),
            (TB, 2), (TB, 6), (TB,), (1,)])
        qhl, khl = carve(rbuf, [(2, 2, 2, C), (2, 2, C)])
        xin, xst, cosT, sinT, ropeA, ropeB, roped, vst = carve(fbuf, [
            (2, TB, E), (KT, C), (T,), (T,), (C,), (C,), (C,), (TB, P)])
        qst, kst = carve(rbuf, [(2, 2, MAPS, C), (2, 2, T)])
        probs, otsb, ot_e, attn_st = carve(fbuf, [(PRING, C), (C,), (16, VD), (2, TB, 2 * VD)])
        vu = fbuf[:, 8192:8704].rearrange("p (a k d) -> p a k d", a=2, k=8)
        mx = sb("mx", [P, 2, 2, 16])
        mparts = sb("mparts", [P, 2, 2, 16], F32R)
        mrows = sb("mrows", [32, 2, P], F32R)
        rec = sb("rec", [P, 16])
        xh, xl, hh, hl, uh, ul = carve(rbuf, [(2, KT, C), (2, KT, C), (KT, C), (KT, C), (2, KT, C), (2, KT, C)])
        h32, su, ysb, sq, rs, xc = carve(fbuf, [(2, KT, C), (2, KT, C), (KT, C), (KT, C), (C,), (2, KT, C)])
        ain, xres, aT, gT, sgT, sT, dsq, dss, dsd, dfin = carve(fbuf, [
            (TB, E), (TB, E), (KT, C), (KT, C), (KT, C), (KT, C), (TB * E,), (TB * E // VD,), (TB * E // VD,), (TB * E // VD,)])

        rt = sb("rt", [32, 2048])
        rw = sb("rw", [P, KT, 32])

        def carve32(sizes):
            views, at = [], 0
            for shape in sizes:
                n = int(np.prod(shape))
                v = rt[:, at:at + n]
                at += n
                names = "abcd"[:len(shape)]
                if len(shape) > 1:
                    v = v.rearrange(f"p ({' '.join(names)}) -> p {' '.join(names)}",
                                    **dict(zip(names, shape)))
                views.append(v)
            assert at <= 2048, at
            return views

        (rb, gb, upper, thr, lgt, gg, biased, cmp, r1, r2, sel, wgt, rsum, bdst) = carve32([
            (LAYERS, NEXP), (LAYERS, NEXP), (NEXP, NEXP), (NEXP,), (16, 32), (16, NEXP), (16, NEXP),
            (16, NEXP, NEXP), (16, NEXP), (16, NEXP), (16, NEXP), (16, NEXP), (16,), (E,)])
        lgT = cmp.rearrange("p a b c -> p (a b c)")[:, 0:C]

        ps = ctx.enter_context(nc.psum_tensor("ps", [P, 8, 512], F32))

        consts_in = sem("consts_in")
        wraw_in = sem("wraw_in")
        consts_ready = sem("consts_ready")
        wproj_ready = sem("wproj_ready")
        dve_consts = sem("dve_consts")
        act_consts = sem("act_consts")
        dve_step = sem("dve_step")
        act_step = sem("act_step")
        pool_step = sem("pool_step")
        wstage_in = sem("wstage_in")
        ffn_w_ready = sem("ffn_w_ready")

        a_xin = [sem(f"a_xin{h}") for h in range(2)]
        a_stats, a_sd = sem("a_stats"), sem("a_sd")
        a_normed, a_transposed, a_xt = sem("a_normed"), sem("a_transposed"), sem("a_xt")
        a_proj_q, a_proj_k, a_proj_v = sem("a_proj_q"), sem("a_proj_k"), sem("a_proj_v")
        a_roped, a_split, a_vst = sem("a_roped"), sem("a_split"), sem("a_vst")
        a_qk_out = [sem(f"a_qk_out{h}") for h in range(2)]
        a_v_out = sem("a_v_out")

        b_zero = sem("b_zero")
        b_qk_in = [[sem(f"b_qk_in{p}{h}") for h in range(2)] for p in range(2)]
        b_v_in = [sem(f"b_v_in{p}") for p in range(2)]
        b_shift_in = [[sem(f"b_shift_in{p}{h}") for h in range(2)] for p in range(2)]
        b_scores, b_exp, b_pv = sem("b_scores"), sem("b_exp"), sem("b_pv")
        b_maxs, b_maxed = sem("b_maxs"), sem("b_maxed")
        b_mparts, b_mturned, b_mrows = sem("b_mparts"), sem("b_mturned"), sem("b_mrows")
        b_ot_out, b_ot_turned, b_ot_read, b_attn = (
            sem("b_ot_out"), sem("b_ot_turned"), sem("b_ot_read"), sem("b_attn"))
        b_attn_out = [sem(f"b_attn_out{h}") for h in range(2)]

        x_stored = sem("x_stored")
        c_xin = [sem(f"c_xin{h}") for h in range(2)]
        c_xh, c_xl, c_up, c_h32, c_hl = (
            sem("c_xh"), sem("c_xl"), sem("c_up"), sem("c_h32"), sem("c_hl"))
        c_gate, c_silu, c_wb, c_u = sem("c_gate"), sem("c_silu"), sem("c_wb"), sem("c_u")
        c_uh, c_ul, c_down, c_y, c_sq = sem("c_uh"), sem("c_ul"), sem("c_down"), sem("c_y"), sem("c_sq")
        c_ms, c_msread, c_ln, c_rs, c_xnew = sem("c_ms"), sem("c_msread"), sem("c_ln"), sem("c_rs"), sem("c_xnew")
        c_logits, c_logits_read, c_lg, c_re, c_wT = (
            sem("c_logits"), sem("c_logits_read"), sem("c_lg"), sem("c_re"), sem("c_wT"))

        d_gin = sem("d_gin")
        d_in, d_sq, d_ss, d_sd, d_an, d_turned, d_aT = (
            sem("d_in"), sem("d_sq"), sem("d_ss"), sem("d_sd"), sem("d_an"), sem("d_turned"), sem("d_aT"))
        d_proj, d_silu, d_s, d_back, d_fin, d_out = (
            sem("d_proj"), sem("d_silu"), sem("d_s"), sem("d_back"), sem("d_fin"), sem("d_out"))

        block = ctx.enter_context(nc.Block())
        N_CONSTS = 23
        FFN_W_STEPS = 2 * NW + 2

        @block.sync
        def _(sp):
            sp.dma_start(wstage[:, 0, :].rearrange("p (k n) -> p k n", k=KT),
                         t["L0_attn_Wq"].rearrange("(k p) n -> p k n", p=P)).then_inc(wraw_in, 16)
            sp.dma_start(wstage[:, 1, 0:KT * P].rearrange("p (k n) -> p k n", k=KT),
                         t["L0_attn_Wk"].rearrange("(k p) n -> p k n", p=P)).then_inc(wraw_in, 16)
            x_v = t["L0_attn_x"].rearrange("b (h k p) e -> h b p k e", h=2, p=P)
            for h in range(2):
                sp.dma_start(xin[:, h], x_v[h, 0]).then_inc(a_xin[h], 16)
            n = 0

            def load(dst, src):
                nonlocal n
                n += 1
                sp.dma_start(dst, src).then_inc(consts_in, 16)

            load(wv[:, :, :], t["L0_attn_Wv"].rearrange("(k p) n -> p k n", p=P))
            load(cosT, t["rope_cos"])
            load(sinT, t["rope_sin"])
            load(sgn, t["rope_sign"])
            load(wo[:, :, :], t["L0_attn_Wo"].rearrange("(k p) n -> p k n", p=P))
            for i, name in enumerate(("q1", "k1", "q2", "k2")):
                load(lamv[:, i], t["L0_attn_lambda_" + name].partition_broadcast(P))
            with nc.allow_non_contiguous_dma("small bias tables"):
                for k in range(KT):
                    load(bup[:, 0:NEXP, k], t["L0_ffn_exp_bup"][:, k * P:(k + 1) * P].rearrange("e p -> p e"))
                    load(bg[:, 0:NEXP, k], t["L0_ffn_exp_bg"][:, k * P:(k + 1) * P].rearrange("e p -> p e"))
                    load(nw[:, :, k], t["L0_ffn_norm_w"][:, k * P:(k + 1) * P].rearrange("j p -> p j"))
                load(bup[:, NEXP:NE, :].rearrange("p e k -> p (e k)"),
                     t["L0_ffn_share_bup"].rearrange("(e p) -> p e", p=P))
                load(bg[:, NEXP, :], t["L0_ffn_share_bg"].rearrange("(k p) -> p k", p=P))
                load(bds, t["L0_ffn_share_bdown"].rearrange("(k p) -> p k", p=P))
                load(rmsw, t["L0_attn_rms_w"].partition_broadcast(P // VD).unsqueeze(2))
            load(rb, t["L0_ffn_router_b"].partition_broadcast(32))
            load(gb, t["L0_ffn_gate_bias"].partition_broadcast(32))
            load(upper, t["upper"].partition_broadcast(32))
            load(thr, t["thr"].partition_broadcast(32))
            assert n == N_CONSTS, n

            def stores(b, h):
                c1 = 2 * b + h + 1
                sp.wait_ge(a_xt, KT * c1)
                sp.dma_start(x_scr[c1 - 1], xst).then_inc(x_stored, 16)
                sp.wait_ge(a_split, 3 * c1)
                t0 = C * h
                for a in range(2):
                    for part in range(2):
                        d = q_scr[part].rearrange("(d a) (b g) m t -> a d b (g m) t", a=2, b=B)
                        sp.dma_start(d[a, :, b, :, t0:t0 + C].bitcast(F32),
                                     qhl[:, h, a, part].bitcast(F32)).then_inc(a_qk_out[h], 16)
                for part in range(2):
                    d = k_scr[:, part].rearrange("d (b g) s t -> d b (g s) t", b=B)
                    sp.dma_start(d[:, b, :, t0:t0 + C].bitcast(F32),
                                 khl[:, h, part].bitcast(F32)).then_inc(a_qk_out[h], 16)
                sp.wait_ge(a_vst, c1)
                for k in range(TB):
                    d = v_scr[b, :, t0 + k * P:t0 + (k + 1) * P, :].rearrange("g p d -> p g d")
                    sp.dma_start(d, vst[:, k].rearrange("p (g d) -> p g d", g=KVH)).then_inc(a_v_out, 16)

            with sp.Fori(0, B - 1) as b:
                for h in range(2):
                    sp.wait_ge(a_transposed, 2 * b + h + 1)
                    sp.dma_start(xin[:, h], x_v[h, b + 1]).then_inc(a_xin[h], 16)
                    stores(b, h)
            for h in range(2):
                stores(B - 1, h)

            for h in range(2):
                sp.wait_ge(a_qk_out[h], 16 * 6 * B)
            sp.wait_ge(a_v_out, 16 * TB * NCH)
            sp.wait_ge(b_zero, 1)
            sp.wait_ge(consts_ready, 9)

            def load_qk(u, par):
                for h in range(2):
                    ts = slice(C * h, C * (h + 1))
                    for r in range(2):
                        sp.dma_start(qst[r:32:2, par, h].bitcast(F32),
                                     q_scr[:, :, u, :, ts].rearrange("a d m t -> (a d) m t").bitcast(F32)
                                     ).then_inc(b_qk_in[par][h], 16)
                        sp.dma_start(kst[16 * r:16 * r + 16, par, :, ts].bitcast(F32),
                                     k_scr[:, :, u, :, ts].rearrange("d a s t -> (d a) s t").bitcast(F32)
                                     ).then_inc(b_qk_in[par][h], 16)

            def load_v(u, par):
                vv = v_scr.rearrange("b g (k p) d -> (b g) p k d", p=P)
                sp.dma_start(vu[:, par, :, 0:VD], vv[u]).then_inc(b_v_in[par], 16)

            def store_shift(u, par, h):
                sp.wait_ge(b_mrows, 2 * u + h + 1)
                sp.dma_start(qst[ZROWS:SROWS, par, h].rearrange("r m t -> r (m t)").bitcast(F32),
                             mrows[:, h].bitcast(F32)).then_inc(b_shift_in[par][h], 16)

            def store_attn(u, h):
                sp.wait_ge(b_attn, 2 * u + h + 1)
                sp.dma_start(a_scr[u, TB * h:TB * (h + 1)].rearrange("k p d -> p k d"),
                             attn_st[:, h]).then_inc(b_attn_out[h], 16)

            def unit(u, par, first, last):
                if not last:
                    if not first:
                        sp.wait_ge(b_scores, JOBS * u)
                    load_qk(u + 1, 1 - par)
                    if not first:
                        sp.wait_ge(b_pv, JOBS * u)
                    load_v(u + 1, 1 - par)
                store_shift(u, par, 1)
                if not first:
                    store_attn(u - 1, 1)
                store_attn(u, 0)
                if not last:
                    store_shift(u + 1, 1 - par, 0)

            load_qk(0, 0)
            load_v(0, 0)
            store_shift(0, 0, 0)
            unit(0, 0, True, False)
            with sp.Fori(0, UNITS // 2 - 1) as i:
                unit(2 * i + 1, 1, False, False)
                unit(2 * i + 2, 0, False, False)
            unit(UNITS - 1, 1, False, True)
            store_attn(UNITS - 1, 1)

            total = LAYERS * NCH
            sp.wait_ge(x_stored, 16 * NCH)
            sp.wait_ge(b_exp, JOBS * UNITS)
            sp.wait_ge(b_pv, JOBS * UNITS)
            sp.wait_ge(b_ot_turned, 2 * UNITS)
            for h in range(2):
                sp.wait_ge(b_attn_out[h], 16 * UNITS)

            def load_state(c, x, par):
                sp.dma_start(xc[:, par], x_scr[x]).then_inc(c_xin[par], 16)

            def c_turn(cc, par):
                sp.wait_ge(x_stored, 16 * (NCH + cc))
                sp.wait_ge(c_y, 2 * cc + 2)
                load_state(cc + 2, (cc + 2) % NCH, par)
                sp.wait_ge(c_xnew, 2 * cc + 2)
                sp.dma_start(x_scr[cc % NCH], ysb).then_inc(x_stored, 16)

            load_state(0, 0, 0)
            load_state(1, 1, 1)
            with sp.Fori(0, total // 2 - 1) as i:
                c_turn(2 * i, 0)
                c_turn(2 * i + 1, 1)
            for cc in range(total - 2, total):
                sp.wait_ge(c_xnew, 2 * cc + 2)
                sp.dma_start(x_scr[cc % NCH], ysb).then_inc(x_stored, 16)

            sp.wait_ge(x_stored, 16 * (NCH + total))
            xr = t["L0_attn_x"].rearrange("b (h k p) e -> (b h) p k e", h=2, p=P)
            ov = out.rearrange("b (h k p) e -> (b h) p k e", h=2, p=P)
            av = a_scr.rearrange("(b g) (h k) p d -> b h g p k d", b=B, h=2)

            def d_load(b, h):
                for g in range(KVH):
                    sp.dma_start(ain[:, :, 32 * g:32 * g + 32], av[b, h, g]).then_inc(d_in, 16)

            def d_chunk(b, h, first):
                c = 2 * b + h
                if not first:
                    sp.wait_ge(d_turned, c)
                d_load(b, h)
                if not first:
                    sp.wait_ge(d_silu, KT * c)
                sp.dma_start(gT, x_scr[c]).then_inc(d_gin, 16)
                if not first:
                    sp.wait_ge(d_out, 16 * c)
                sp.dma_start(xres, xr[c]).then_inc(d_in, 16)
                sp.wait_ge(d_fin, 2 * c + 2)
                sp.dma_start(ov[c], xres).then_inc(d_out, 16)

            d_chunk(0, 0, True)
            d_chunk(0, 1, False)
            with sp.Fori(1, B) as b:
                d_chunk(b, 0, False)
                d_chunk(b, 1, False)
            sp.wait_ge(d_out, 16 * NCH)

        @block.gpsimd
        def _(pool):
            st = Steps(pool, pool_step)
            st.done(pool.memset(ident[:, :], 0.0))
            st.done(pool.memset(identb[:, :], 0.0))
            st.done(pool.memset(maskq[:, :], 0.0))
            st.done(pool.memset(maskk[:, :], 0.0))
            st.done(pool.memset(selw[:, :, :].bitcast(F32), 0.0))
            pool.memset(meanw[:, :], 1.0 / E).then_inc(consts_ready, 1)
            pool.memset(rw[:, :, :], 0.0).then_inc(consts_ready, 1)
            pool.memset(whl[:, :, :].bitcast(F32), 0.0).then_inc(consts_ready, 1)
            pool.memset(bdr[:, :, :].bitcast(F32), 0.0).then_inc(consts_ready, 1)
            st.done(pool.memset(vu[:, :, :, :], 0.0))
            st.wait()
            pool.affine_select(out=ident[:, :], in_=ident[:, :], pattern=[[-1, P]], compare_op=ALU.not_equal,
                               fill=1.0, base=0, channel_multiplier=1).then_inc(consts_ready, 1)
            pool.affine_select(out=identb[:, :], in_=identb[:, :], pattern=[[-1, P]], compare_op=ALU.not_equal,
                               fill=1.0, base=0, channel_multiplier=1).then_inc(consts_ready, 1)
            pool.affine_select(out=maskq[:, :], in_=maskq[:, :], pattern=[[-1, P]], compare_op=ALU.is_ge,
                               fill=NEG, base=0, channel_multiplier=1).then_inc(consts_ready, 1)
            pool.affine_select(out=maskk[:, :], in_=maskk[:, :], pattern=[[1, P]], compare_op=ALU.is_ge,
                               fill=NEG, base=0, channel_multiplier=-1).then_inc(consts_ready, 1)
            for off in (0, NEXP):
                st.done(pool.affine_select(out=selw[:, :, :], in_=selw[:, :, :].bitcast(F32),
                                           pattern=[[-1, NEXP], [0, P]], compare_op=ALU.not_equal,
                                           fill=1.0, base=-off, channel_multiplier=1))
                st.wait()
            pool.memset(vu[:, :, :, VD:VD + 1], 1.0).then_inc(consts_ready, 1)
            pool.wait_ge(wraw_in, 32)
            for k in range(KT):
                raw = wstage[:, 0, k * E:(k + 1) * E].rearrange("p (h a d) -> p a d h", a=2, d=4)
                for a in range(2):
                    pool.tensor_copy(wq[:, k, a].rearrange("p (d h) -> p d h", d=4), raw[:, a]
                                     ).then_inc(wproj_ready, 1)
                raw = wstage[:, 1, k * P:(k + 1) * P].rearrange("p (h a d) -> p a d h", a=2, d=4)
                for s in range(2):
                    dst = wk[:, k, s].rearrange("p (d a h) -> p a d h", d=4, a=2)
                    for a in range(2):
                        pool.tensor_copy(dst[:, a], raw[:, a ^ s]).then_inc(wproj_ready, 1)

            up = t["L0_ffn_exp_Wup"].rearrange("e (k p) n -> e p k n", p=P)
            gate = t["L0_ffn_exp_Wg"].rearrange("e (k p) n -> e p k n", p=P)
            down = t["L0_ffn_exp_Wdown"].rearrange("e (k p) n -> e p k n", p=P)
            pool.wait_ge(wproj_ready, 12)

            def split(i, turn, slot, src, w, first):
                dst = wstage[:, slot].rearrange("p (k n) -> p k n", k=KT)
                pool.dma_start(dst, src).then_inc(wstage_in, 16)
                pool.wait_ge(wstage_in, 16 * (turn + 1))
                pool.tensor_copy(WH[:, w], wstage[:, slot]).then_inc(ffn_w_ready, 1)
                pool.wait_ge(ffn_w_ready, 2 * turn + 1)
                pool.tensor_tensor(WL[:, w], wstage[:, slot], WH[:, w].bitcast(F32), ALU.subtract
                                   ).then_inc(ffn_w_ready, 1)
                pool.wait_ge(ffn_w_ready, 2 * turn + 2)

            for e in range(NEXP):
                for j, (m, w0) in enumerate(((up, W_UP), (gate, W_GATE), (down, W_DOWN))):
                    n = 3 * e + j
                    split(e, n, n % 2, m[e], w0 + e, n < 2)
            share = [(t["L0_ffn_share_Wup"][:, E * s:E * (s + 1)], W_UP + NEXP + s) for s in range(NSH)]
            share += [(t["L0_ffn_share_Wg"], W_GATE + NEXP), (t["L0_ffn_share_Wdown"], W_DOWN + NEXP)]
            for j, (m, w) in enumerate(share):
                split(0, 3 * NEXP + j, j % 2, m.rearrange("(k p) n -> p k n", p=P), w, False)
            with nc.allow_non_contiguous_dma("router weights"):
                pool.wait_ge(consts_ready, 9)
                for j in range(LAYERS):
                    pool.dma_start(rw[:, :, NEXP * j:NEXP * (j + 1)],
                                   t["L0_ffn_router_W"][j].rearrange("(k p) e -> p k e", p=P)).then_inc(wstage_in, 16)
            pool.dma_start(bdst[0:NEXP], t["L0_ffn_exp_bdown"]).then_inc(wstage_in, 16)
            pool.dma_start(bdst[NEXP:2 * NEXP], t["L0_ffn_exp_bdown"]).then_inc(wstage_in, 16)
            pool.wait_ge(wstage_in, 16 * (NW + 4))
            pool.tensor_copy(bdr[0:2 * NEXP, 0], bdst[0:2 * NEXP]).then_inc(ffn_w_ready, 1)
            pool.wait_ge(ffn_w_ready, FFN_W_STEPS - 1)
            pool.tensor_tensor(bdr[0:2 * NEXP, 1], bdst[0:2 * NEXP], bdr[0:2 * NEXP, 0].bitcast(F32),
                               ALU.subtract).then_inc(ffn_w_ready, 1)

        @block.tensor
        def _(pe):
            def proj_chunk(b, h, first):
                c = 2 * b + h
                c0 = C * c
                pe.wait_ge(a_normed, TB * (c + 1))
                if not first:
                    pe.wait_ge(a_xt, KT * c)
                for m in range(KT):
                    for k in range(TB):
                        last = pe.transpose(ps[:, m, k * P:(k + 1) * P], xin[:, h, k, m * P:(m + 1) * P], ident[:, :])
                last.then_inc(a_transposed, 1)
                pe.wait_ge(a_xt, KT * (c + 1))
                if not first:
                    pe.wait_ge(a_roped, 3 * c)
                for a in range(2):
                    for k in range(KT):
                        last = pe.matmul(ps[:, 2 + a, :], wq[:, k, a], xst[:, k], start=(k == 0), stop=(k == KT - 1))
                last.then_inc(a_proj_q, 1)
                for s in range(2):
                    for k in range(KT):
                        last = pe.matmul(ps[:, 4 + s, :], wk[:, k, s], xst[:, k], start=(k == 0), stop=(k == KT - 1))
                last.then_inc(a_proj_k, 1)
                if not first:
                    pe.wait_ge(a_vst, c)
                for tb in range(TB):
                    for k in range(KT):
                        last = pe.matmul(ps[:, 6, tb * P:(tb + 1) * P], xst[:, k, tb * P:(tb + 1) * P], wv[:, k],
                                         start=(k == 0), stop=(k == KT - 1))
                last.then_inc(a_proj_v, 1)

            pe.wait_ge(consts_ready, 9)
            pe.wait_ge(wproj_ready, 12)
            pe.wait_ge(consts_in, 16 * N_CONSTS)
            proj_chunk(0, 0, True)
            proj_chunk(0, 1, False)
            with pe.Fori(1, B) as b:
                proj_chunk(b, 0, False)
                proj_chunk(b, 1, False)

            pe.wait_ge(a_roped, 3 * NCH)
            pe.wait_ge(a_vst, NCH)
            pe.wait_ge(a_xt, KT * NCH)
            ST, MX, OT, TR = 0, 2, 6, 7

            def max_matmul(u, par, s, first=False):
                pair, w = s // 2, s % 2
                i, piece, mp = MAXP[pair]
                if s == 0:
                    pe.wait_ge(b_qk_in[par][0], 64 * (u // 2 + 1))
                if pair == MAXA and w == 0:
                    pe.wait_ge(b_qk_in[par][1], 64 * (u // 2 + 1))
                if w == 0 and not (first and pair < 2):
                    pe.wait_ge(b_maxed, len(MAXP) * u + pair - 1)
                m = 2 * mp + w
                width = min(512, P * (i + 1) - 512 * piece)
                o = ps[:, MX + 2 * (pair % 2) + w, 0:width]
                diag = piece == i // 4
                ins = pe.matmul(o, qst[0:ZROWS, par, i // 4, m, P * (i % 4):P * (i % 4 + 1)],
                                kst[0:ZROWS, par, m % 2, 512 * piece:512 * piece + width],
                                start=True, stop=not diag)
                if diag:
                    ins = pe.matmul(o[:, width - P:width], identb[:, :], maskq[:, :], start=False, stop=True)
                if w == 1:
                    ins.then_inc(b_maxs, 1)

            def scores(u, par, s, first):
                (h, j), m = GROUPS[s // MAPS], s % MAPS
                if s in (0, MAPS * 4):
                    pe.wait_ge(b_shift_in[par][h], 16 * (u // 2 + 1))
                if not (first and s < 2):
                    pe.wait_ge(b_exp, JOBS * u + s - 1)
                t0 = max(0, P * j - C * h)
                o = ps[:, ST + s % 2, t0:C]
                diag = P * j >= C * h
                ins = pe.matmul(o, kst[0:SROWS, par, m % 2, P * j:P * (j + 1)], qst[0:SROWS, par, h, m, t0:C],
                                start=True, stop=not diag)
                if diag:
                    ins = pe.matmul(o[:, 0:P], identb[:, :], maskk[:, :], start=False, stop=True)
                ins.then_inc(b_scores, 1)

            def values(u, par, s, first):
                (h, j), m = GROUPS[s // MAPS], s % MAPS
                if s == 0:
                    pe.wait_ge(b_v_in[par], 16 * (u // 2 + 1))
                if s in (0, MAPS * 4) and not (first and s == 0):
                    pe.wait_ge(b_ot_out, 2 * u + h)
                pe.wait_ge(b_exp, JOBS * u + s + 1)
                t0 = max(0, P * j - C * h)
                pe.matmul(ps[32 * m:32 * m + 32, OT, t0:C], vu[:, par, j, :], probs[:, s % PRING, t0:C],
                          start=(j == 0), stop=(j == 4 * h + 3)).then_inc(b_pv, 1)

            def turn_shift(u, h):
                pe.wait_ge(b_mparts, 2 * (2 * u + h) + 2)
                pe.transpose(ps[0:32, TR, 0:P], mparts[:, h].rearrange("p a n -> p (a n)").bitcast(F32),
                             ident[:, :]).then_inc(b_mturned, 1)

            def turn_ot(u, h):
                pe.wait_ge(b_ot_out, 2 * u + h + 1)
                for k in range(TB):
                    ins = pe.transpose(ps[:, TR, k * P:(k + 1) * P], otsb[:, k * P:(k + 1) * P], ident[:, :])
                ins.then_inc(b_ot_turned, 1)

            def unit(u, par, first, last):
                for s in range(JOBS):
                    scores(u, par, s, first)
                    if s < JOBS - LEAD:
                        max_matmul(u, par, s + LEAD)
                    elif not last:
                        max_matmul(u + 1, 1 - par, s + LEAD - JOBS)
                    if s % MAPS == VALUES_AT:
                        for m in range(MAPS):
                            if s >= MAPS:
                                values(u, par, s - VALUES_AT - MAPS + m, first)
                            elif not first:
                                values(u - 1, 1 - par, JOBS - MAPS + m, False)
                    if s == SHIFT_B_AT:
                        pe.wait_ge(b_mrows, 2 * u + 1)
                        turn_shift(u, 1)
                    if s == OT_B_AT and not first:
                        pe.wait_ge(b_mrows, 2 * u + 2)
                        turn_ot(u - 1, 1)
                    if s == OT_A_AT:
                        if first:
                            pe.wait_ge(b_mrows, 2)
                        else:
                            pe.wait_ge(b_ot_read, 2 * u)
                        turn_ot(u, 0)
                    if s == SHIFT_A_AT and not last:
                        pe.wait_ge(b_ot_read, 2 * u + 1)
                        turn_shift(u + 1, 0)

            for s in range(LEAD):
                max_matmul(0, 0, s, True)
                if s == 2 * MAXA + 4:
                    turn_shift(0, 0)
            unit(0, 0, True, False)
            with pe.Fori(0, UNITS // 2 - 1) as i:
                unit(2 * i + 1, 1, False, False)
                unit(2 * i + 2, 0, False, False)
            unit(UNITS - 1, 1, False, True)
            for s in range(JOBS - MAPS, JOBS):
                values(UNITS - 1, 1, s, False)
            pe.wait_ge(b_ot_read, 2 * UNITS - 1)
            turn_ot(UNITS - 1, 1)

            HB, ZB, YB, WB, LB = 0, 2, 4, 6, 7
            pe.wait_ge(b_exp, JOBS * UNITS)
            pe.wait_ge(b_maxed, len(MAXP) * UNITS)
            pe.wait_ge(b_ot_read, 2 * UNITS)
            pe.wait_ge(ffn_w_ready, FFN_W_STEPS)

            def product(o, w, m, hi, lo, start, stop):
                n = 0
                for k in range(KT):
                    cols = slice(E * k + P * m, E * k + P * (m + 1))
                    for ww, xx in ((WH, hi), (WL, hi), (WH, lo)):
                        ins = pe.matmul(o, ww[:, w, cols], xx[:, k], start=(start and n == 0),
                                        stop=(stop and n == 3 * KT - 1))
                        n += 1
                return ins

            def up(cc, e, par, first=False):
                G = NE * cc + e
                if e == 0:
                    pe.wait_ge(c_xl, KT * (cc + 1))
                for m in range(KT):
                    if not first:
                        pe.wait_ge(c_h32, 2 * G - 1 + m)
                    product(ps[:, HB + m], W_UP + e, m, xh[:, par], xl[:, par], True, True).then_inc(c_up, 1)

            def gate(cc, e, first=False):
                G = NE * cc + e
                pe.wait_ge(c_hl, 2 * G + 2)
                for m in range(KT):
                    if not first:
                        pe.wait_ge(c_silu, 2 * G - 2 + m + 1)
                    product(ps[:, ZB + m], W_GATE + min(e, NEXP), m, hh, hl, True, True).then_inc(c_gate, 1)

            def down_bias(cc, par, first=False):
                if not first:
                    pe.wait_ge(c_y, 2 * cc)
                for m in range(KT):
                    for part in range(2):
                        pe.matmul(ps[:, YB + m], bdr[:, part, P * m:P * (m + 1)], wT[:, par],
                                  start=(part == 0), stop=False)

            def down(cc, d, par):
                D = (NEXP + 1) * cc + d
                dp = (par + d) % 2
                pe.wait_ge(c_ul, 2 * D + 2)
                for m in range(KT):
                    ins = product(ps[:, YB + m], W_DOWN + d, m, uh[:, dp], ul[:, dp], False, d == NEXP)
                ins.then_inc(c_down, 1)

            def expert_weight(cc, e, par, first=False):
                if e == 0:
                    pe.wait_ge(c_wT, cc + 1)
                if not first:
                    pe.wait_ge(c_u, 2 * (NE * cc + (e if e else -1)))
                pe.matmul(ps[:, WB], selw[:, e], wT[:, par], start=True, stop=True).then_inc(c_wb, 1)

            def route(cc, par):
                pe.wait_ge(c_xin[par], 16 * (cc // 2 + 1))
                for k in range(KT):
                    ins = pe.matmul(ps[0:32, LB, :], rw[:, k, :], xc[:, par, k], start=(k == 0), stop=(k == KT - 1))
                ins.then_inc(c_logits, 1)

            def mean_square(cc):
                pe.wait_ge(c_sq, 2 * cc + 2)
                for m in range(KT):
                    ins = pe.matmul(ps[:, LB], meanw[:, :], sq[:, m], start=(m == 0), stop=(m == KT - 1))
                ins.then_inc(c_ms, 1)

            def chunk(cc, par, first, last):
                for e in range(NE):
                    if e < NE - 1:
                        up(cc, e + 1, par)
                    elif not last:
                        up(cc + 1, 0, 1 - par)
                    if e == 0 and not first:
                        down(cc - 1, NEXP, 1 - par)
                    if e == 1:
                        down_bias(cc, par, first)
                        if not first:
                            pe.wait_ge(c_logits_read, cc + 1)
                            mean_square(cc - 1)
                    if e > 1:
                        down(cc, e - 2, par)
                    if e < NE - 1:
                        gate(cc, e + 1)
                    elif not last:
                        gate(cc + 1, 0)
                    if e + 1 < NEXP:
                        expert_weight(cc, e + 1, par)
                    elif e == NE - 1 and not last:
                        expert_weight(cc + 1, 0, 1 - par)
                    if e == 2 and not last:
                        if not first:
                            pe.wait_ge(c_msread, cc)
                        route(cc + 1, 1 - par)

            route(0, 0)
            up(0, 0, 0, True)
            gate(0, 0, True)
            expert_weight(0, 0, 0, True)
            chunk(0, 0, True, False)
            total = LAYERS * NCH
            with pe.Fori(0, total // 2 - 1) as i:
                chunk(2 * i + 1, 1, False, False)
                chunk(2 * i + 2, 0, False, False)
            chunk(total - 1, 1, False, True)
            down(total - 1, NEXP, 1)
            mean_square(total - 1)

            pe.wait_ge(c_y, 2 * total)

            def d_chunk(c, first):
                pe.wait_ge(d_an, c + 1)
                if not first:
                    pe.wait_ge(d_aT, 2 * c)
                for m in range(KT):
                    for k in range(TB):
                        last = pe.transpose(ps[:, m, k * P:(k + 1) * P], ain[:, k, m * P:(m + 1) * P], ident[:, :])
                last.then_inc(d_turned, 1)
                pe.wait_ge(d_aT, 2 * c + 2)
                if not first:
                    pe.wait_ge(d_s, 2 * c)
                for m in range(KT):
                    for k in range(KT):
                        last = pe.matmul(ps[:, 2 + m], wo[:, k, m * P:(m + 1) * P], aT[:, k],
                                         start=(k == 0), stop=(k == KT - 1))
                last.then_inc(d_proj, 1)
                pe.wait_ge(d_s, 2 * c + 2)
                if not first:
                    pe.wait_ge(d_fin, 2 * c)
                for k in range(TB):
                    for m in range(KT):
                        last = pe.transpose(ps[:, 4 + k // 2, (k % 2) * E + m * P:(k % 2) * E + (m + 1) * P],
                                            sT[:, m, k * P:(k + 1) * P], ident[:, :])
                last.then_inc(d_back, 1)

            pe.wait_ge(dve_consts, 1)
            d_chunk(0, True)
            with pe.Fori(1, NCH) as c:
                d_chunk(c, False)

        @block.scalar
        def _(act):
            st = Steps(act, act_step)
            act.wait_ge(dve_consts, 1)
            act.activation(lame, lams, ACT.Exp).then_inc(act_consts, 1)

            def proj_chunk(b, h, first):
                c = 2 * b + h
                act.wait_ge(a_stats, c + 1)
                act.activation(rst, mv[:, :, 1], ACT.Sqrt).then_inc(a_sd, 1)
                act.wait_ge(a_transposed, c + 1)
                if not first:
                    act.wait_ge(a_proj_v, c)
                    act.wait_ge(x_stored, 16 * c)
                for m in range(KT):
                    act.copy(xst[:, m], ps[:, m]).then_inc(a_xt, 1)
                act.wait_ge(a_proj_v, c + 1)
                if not first:
                    act.wait_ge(a_v_out, 16 * TB * c)
                act.copy(vst.rearrange("p k n -> p (k n)"), ps[:, 6]).then_inc(a_vst, 1)

            proj_chunk(0, 0, True)
            proj_chunk(0, 1, False)
            with act.Fori(1, B) as b:
                proj_chunk(b, 0, False)
                proj_chunk(b, 1, False)

            act.wait_ge(a_split, 3 * NCH)
            act.wait_ge(a_v_out, 16 * TB * NCH)
            act.wait_ge(a_transposed, NCH)

            def ot_evacuate(u, h):
                act.wait_ge(b_pv, JOBS * u + (16 if h == 0 else JOBS))
                if not (isinstance(u, int) and u == 0 and h == 0):
                    act.wait_ge(b_ot_turned, 2 * u + h)
                act.copy(otsb, ps[:, 6]).then_inc(b_ot_out, 1)

            def unit(u, par, first):
                for s in range(JOBS):
                    (h, j), m = GROUPS[s // MAPS], s % MAPS
                    act.wait_ge(b_scores, JOBS * u + s + 1)
                    if m == 0 and not (first and s < PRING):
                        act.wait_ge(b_pv, JOBS * u + s - MAPS)
                    t0 = max(0, P * j - C * h)
                    act.activation(probs[:, s % PRING, t0:C], ps[:, s % 2, t0:C], ACT.Exp, scale=SCALE
                                   ).then_inc(b_exp, 1)
                    if s == OT_EVAC_B_AT and not first:
                        ot_evacuate(u - 1, 1)
                    if s == OT_EVAC_A_AT:
                        ot_evacuate(u, 0)

            unit(0, 0, True)
            with act.Fori(0, UNITS // 2 - 1) as i:
                unit(2 * i + 1, 1, False)
                unit(2 * i + 2, 0, False)
            unit(UNITS - 1, 1, False)
            ot_evacuate(UNITS - 1, 1)

            act.wait_ge(b_ot_turned, 2 * UNITS)
            act.wait_ge(b_attn, 2 * UNITS)
            act.wait_ge(ffn_w_ready, FFN_W_STEPS)

            def split_x(cc, par, first):
                act.wait_ge(c_xin[par], 16 * (cc // 2 + 1))
                if not first:
                    act.wait_ge(c_up, 2 * NE * (cc - 1))
                for k in range(KT):
                    act.copy(xh[:, par, k], xc[:, par, k]).then_inc(c_xh, 1)

            def hidden(cc, e, gp, first=False):
                G = NE * cc + e
                for m in range(KT):
                    act.wait_ge(c_up, 2 * G + m + 1)
                    if not first and m == 0:
                        act.wait_ge(c_gate, 2 * G)
                    act.activation(hh[:, m], ps[:, m], ACT.Identity, bias=bup[:, e, m:m + 1])
                    if not first:
                        act.wait_ge(c_u, 2 * (G - 2) + m + 1)
                    act.activation(h32[:, gp, m], ps[:, m], ACT.Identity, bias=bup[:, e, m:m + 1]
                                   ).then_inc(c_h32, 1)

            def split_u(cc, d, par, first):
                e = d if d < NEXP else NE - 1
                D = (NEXP + 1) * cc + d
                for m in range(KT):
                    act.wait_ge(c_u, 2 * (NE * cc + e) + m + 1)
                    if m == 0 and not (first and d < 2):
                        act.wait_ge(c_down, D - 1)
                    act.copy(uh[:, (par + d) % 2, m], su[:, e % 2, m]).then_inc(c_uh, 1)

            def chunk(cc, par, first, last):
                for e in range(NE):
                    G = NE * cc + e
                    for m in range(KT):
                        act.wait_ge(c_gate, 2 * G + m + 1)
                        if e == 0:
                            if not first:
                                act.wait_ge(c_u, 2 * G - 1 + m)
                        elif not (first and e == 1):
                            act.wait_ge(c_ul, 2 * ((NEXP + 1) * cc + e - 1) - 1 + m)
                        act.activation(su[:, e % 2, m], ps[:, 2 + m], ACT.Silu,
                                       bias=bg[:, min(e, NEXP), m:m + 1]).then_inc(c_silu, 1)
                    if e == 1 and not first:
                        square(cc - 1, False)
                    if e < NE - 1:
                        hidden(cc, e + 1, (e + 1) % 2, first=first and e == 0)
                    elif not last:
                        hidden(cc + 1, 0, 0)
                    if e == 5:
                        if not first:
                            inv_rms(cc - 1)
                        if not last:
                            route_exp(cc + 1)
                    elif e == 6:
                        split_u(cc, 5, par, first)
                    else:
                        split_u(cc, min(e, NEXP), par, first)
                    if e == 3 and not last:
                        split_x(cc + 1, 1 - par, first)

            def square(cc, first):
                for m in range(KT):
                    act.wait_ge(c_y, 2 * cc + m + 1)
                    act.activation(sq[:, m], ysb[:, m], ACT.Square).then_inc(c_sq, 1)

            def inv_rms(cc):
                act.wait_ge(c_msread, cc + 1)
                act.activation(rs, rs, ACT.Ln, bias=epsn).then_inc(c_ln, 1)
                act.wait_ge(c_ln, cc + 1)
                act.activation(rs, rs, ACT.Exp, scale=-0.5).then_inc(c_rs, 1)

            def route_exp(cc):
                act.wait_ge(c_lg, cc + 1)
                act.activation(wgt, gg, ACT.Exp).then_inc(c_re, 1)

            split_x(0, 0, True)
            route_exp(0)
            hidden(0, 0, 0, first=True)
            chunk(0, 0, True, False)
            total = LAYERS * NCH
            with act.Fori(0, total // 2 - 1) as i:
                chunk(2 * i + 1, 1, False, False)
                chunk(2 * i + 2, 0, False, False)
            chunk(total - 1, 1, False, True)
            square(total - 1, False)
            inv_rms(total - 1)

            def d_chunk(c, first):
                act.wait_ge(d_ss, c + 1)
                act.activation(dsd, dss, ACT.Sqrt).then_inc(d_sd, 1)
                act.wait_ge(d_turned, c + 1)
                if not first:
                    act.wait_ge(d_proj, c)
                for m in range(KT):
                    act.copy(aT[:, m], ps[:, m]).then_inc(d_aT, 1)
                if not first:
                    act.wait_ge(d_s, 2 * c)
                act.wait_ge(d_gin, 16 * (c + 1))
                for m in range(KT):
                    act.activation(sgT[:, m], gT[:, m], ACT.Silu).then_inc(d_silu, 1)

            act.wait_ge(c_xnew, 2 * total)
            d_chunk(0, True)
            with act.Fori(1, NCH) as c:
                d_chunk(c, False)

        @block.vector
        def _(dve):
            st = Steps(dve, dve_step)

            def go(ins):
                st.done(ins)
                st.wait()

            dve.wait_ge(consts_in, 16 * N_CONSTS)
            st.done(dve.memset(epsn, 1e-6))
            for i in range(2):
                st.done(dve.tensor_tensor(lamp[:, i], lamv[:, 2 * i], lamv[:, 2 * i + 1], ALU.mult))
            st.done(dve.tensor_scalar(rmsw, rmsw, 1.0 - LAMBDA_INIT, None, ALU.mult))
            st.done(dve.tensor_scalar(bds, bds, float(NSH), None, ALU.mult))
            st.wait()
            st.done(dve.tensor_reduce(lams, lamp, AX, ALU.add))
            st.wait()
            dve.tensor_scalar(wo[:, :, :].rearrange("p k n -> p (k n)"), wo[:, :, :].rearrange("p k n -> p (k n)"),
                              rmsw, None, ALU.mult).then_inc(dve_consts, 1)
            dve.wait_ge(act_consts, 1)
            go(dve.tensor_tensor(lamneg, lame[:, 1:2], lame[:, 0:1], ALU.subtract))
            go(dve.tensor_scalar(lamneg, lamneg, -LAMBDA_INIT, None, ALU.add))

            def norm_chunk(b, h, bx):
                c = 2 * b + h
                dve.wait_ge(a_xin[h], 16 * (b + 1))
                for k in range(TB):
                    st.done(dve.bn_stats(bst[:, k], xin[:, h, k]))
                st.wait()
                st.done(dve.tensor_copy(rst[:, 0:1], bst[:, 0, 0:1]))
                for k in range(TB):
                    st.done(dve.bn_aggr(mv[:, k], bst[:, k]))
                st.wait()
                dve.tensor_scalar(mv[:, :, 1], mv[:, :, 1], 1e-5, None, ALU.add).then_inc(a_stats, 1)
                dve.wait_ge(a_sd, c + 1)
                go(dve.reciprocal(rst, rst))
                for k in range(TB):
                    dve.tensor_scalar(xin[:, h, k], xin[:, h, k], mv[:, k, 0:1], rst[:, k:k + 1],
                                      ALU.subtract, ALU.mult).then_inc(a_normed, 1)

            def rope_chunk(b, h, first):
                c = 2 * b + h
                ts = slice(C * h, C * (h + 1))
                cs, sn = cosT[:, ts], sinT[:, ts]
                dve.wait_ge(a_proj_q, c + 1)
                if not first:
                    dve.wait_ge(a_qk_out[h], 96 * b)
                for tile in range(3):
                    if tile == 2:
                        dve.wait_ge(a_proj_k, c + 1)
                    one, two = ((2, 3), (3, 2), (4, 5))[tile]
                    st.done(dve.tensor_tensor(ropeA, ps[:, one], cs, ALU.mult))
                    if tile < 2:
                        st.done(dve.tensor_tensor(ropeB, ps[:, two], sn, ALU.mult))
                    else:
                        st.done(dve.scalar_tensor_tensor(ropeB, ps[:, two], sgn, sn, ALU.mult, ALU.mult))
                    st.wait()
                    dve.tensor_tensor(roped, ropeA, ropeB, ALU.subtract if tile == 1 else ALU.add
                                      ).then_inc(a_roped, 1)
                    dve.wait_ge(a_roped, 3 * c + tile + 1)
                    dst = qhl[:, h, tile] if tile < 2 else khl[:, h]
                    go(dve.tensor_copy(dst[:, 0], roped))
                    dve.tensor_tensor(dst[:, 1], roped, dst[:, 0].bitcast(F32), ALU.subtract).then_inc(a_split, 1)
                    dve.wait_ge(a_split, 3 * c + tile + 1)

            def a_body(b, first):
                norm_chunk(b, 0, first)
                rope_chunk(b, 0, first)
                norm_chunk(b, 1, first)
                rope_chunk(b, 1, first)

            a_body(0, True)
            with dve.Fori(1, B) as b:
                st.enter(b - 1, A_STEPS)
                a_body(b, False)
                st.leave(B - 1)

            for h in range(2):
                dve.wait_ge(a_qk_out[h], 96 * B)
            go(dve.memset(qst[:, 0].rearrange("p a m t -> p (a m t)").bitcast(F32), 0.0))
            st.done(dve.memset(qst[:, 1].rearrange("p a m t -> p (a m t)").bitcast(F32), 0.0))
            go(dve.memset(kst.rearrange("p a s t -> p (a s t)").bitcast(F32), 0.0))
            dve.memset(kst[ZROWS:P].rearrange("p a s t -> p (a s t)").bitcast(F32), 1.0).then_inc(b_zero, 1)
            TR = 7

            def reduce_pair(u, pair):
                i, piece, mp = MAXP[pair]
                width = min(512, P * (i + 1) - 512 * piece)
                dve.wait_ge(b_maxs, len(MAXP) * u + pair + 1)
                h = i // 4
                o = mx[:, h, piece].rearrange("p (m i) -> p m i", m=MAPS)[:, 2 * mp:2 * mp + 2, i % 4]
                dve.tensor_reduce(o, ps[:, 2 + 2 * (pair % 2):4 + 2 * (pair % 2), 0:width], AX, ALU.max,
                                  negate=True).then_inc(b_maxed, 1)

            def shift_parts(u, h, par, first):
                dve.wait_ge(b_maxed, len(MAXP) * u + (MAXA if h == 0 else len(MAXP)))
                if h == 1:
                    go(dve.tensor_tensor(mx[:, 1, 0], mx[:, 1, 0], mx[:, 1, 1], ALU.min))
                if not first:
                    dve.wait_ge(b_mturned, 2 * u - 1 + h)
                dve.tensor_copy(mparts[:, h, 0], mx[:, h, 0]).then_inc(b_mparts, 1)
                dve.wait_ge(b_mparts, 2 * (2 * u + h) + 1)
                dve.tensor_tensor(mparts[:, h, 1], mx[:, h, 0], mparts[:, h, 0].bitcast(F32), ALU.subtract
                                  ).then_inc(b_mparts, 1)

            def shift_rows(u, h, par, first):
                dve.wait_ge(b_mturned, 2 * u + h + 1)
                if not first:
                    dve.wait_ge(b_shift_in[1 - par][h], 16 * ((u + 1) // 2))
                dve.tensor_copy(mrows[:, h], ps[0:32, TR, 0:P]).then_inc(b_mrows, 1)

            def combine(u, h, first):
                dve.wait_ge(b_ot_turned, 2 * u + h + 1)
                v = ps[:, TR, :].rearrange("p (n d) -> p n d", d=32)
                go(dve.reciprocal(rec[:, :], v[:, :, VD]))
                r2v = rec[:, :].rearrange("p (n c) -> p n c", c=2)[:, :, 1]
                go(dve.tensor_scalar(r2v, r2v, lamneg, None, ALU.mult))
                dve.tensor_tensor(ot_e, v[:, :, 0:VD], rec[:, :].unsqueeze(2).broadcast_to((P, 16, VD)), ALU.mult
                                  ).then_inc(b_ot_read, 1)
                dve.wait_ge(b_ot_read, 2 * u + h + 1)
                if not first:
                    dve.wait_ge(b_attn_out[h], 16 * u)
                ev = ot_e.rearrange("p (n c) d -> p n c d", c=2)
                dve.tensor_tensor(attn_st[:, h].rearrange("p k (r d) -> p (k r) d", r=2), ev[:, :, 0], ev[:, :, 1],
                                  ALU.add).then_inc(b_attn, 1)

            def unit(u, par, first, last):
                for s in range(JOBS):
                    w = s + LEAD
                    if w < JOBS:
                        if w % 2:
                            reduce_pair(u, w // 2)
                            if w == JOBS - 1:
                                shift_parts(u, 1, par, first)
                    elif not last:
                        w -= JOBS
                        if w % 2:
                            reduce_pair(u + 1, w // 2)
                            if w == 2 * MAXA - 1:
                                shift_parts(u + 1, 0, 1 - par, False)
                    if s == SHIFT_B_AT:
                        shift_rows(u, 1, par, first)
                    if s == OT_B_AT and not first:
                        combine(u - 1, 1, first == 2)
                    if s == OT_A_AT:
                        combine(u, 0, first)
                    if s == SHIFT_A_AT and not last:
                        shift_rows(u + 1, 0, 1 - par, False)

            for s in range(LEAD):
                if s % 2:
                    reduce_pair(0, s // 2)
                if s == 2 * MAXA - 1:
                    shift_parts(0, 0, 0, True)
                if s == 2 * MAXA + 4:
                    shift_rows(0, 0, 0, True)
            unit(0, 0, True, False)
            with dve.Fori(0, UNITS // 2 - 1) as i:
                st.enter(i, B_STEPS)
                unit(2 * i + 1, 1, False, False)
                unit(2 * i + 2, 0, False, False)
                st.leave(UNITS // 2 - 1)
            unit(UNITS - 1, 1, False, True)
            combine(UNITS - 1, 1, False)

            dve.wait_ge(b_scores, JOBS * UNITS)
            dve.wait_ge(b_pv, JOBS * UNITS)
            dve.wait_ge(b_ot_turned, 2 * UNITS)

            def split_x(cc, par):
                for k in range(KT):
                    dve.wait_ge(c_xh, KT * cc + k + 1)
                    dve.tensor_tensor(xl[:, par, k], xc[:, par, k], xh[:, par, k].bitcast(F32), ALU.subtract
                                      ).then_inc(c_xl, 1)

            def hidden_low(cc, e):
                G = NE * cc + e
                for m in range(KT):
                    dve.wait_ge(c_h32, 2 * G + m + 1)
                    dve.tensor_tensor(hl[:, m], h32[:, e % 2, m], hh[:, m].bitcast(F32), ALU.subtract
                                      ).then_inc(c_hl, 1)

            def gated(cc, e, m):
                G = NE * cc + e
                dve.wait_ge(c_silu, 2 * G + m + 1)
                s = su[:, e % 2, m]
                if e < NEXP:
                    go(dve.tensor_tensor(s, s, h32[:, e % 2, m], ALU.mult))
                    dve.wait_ge(c_wb, NEXP * cc + e + 1)
                    dve.tensor_tensor(s, s, ps[:, 6], ALU.mult).then_inc(c_u, 1)
                elif e == NEXP:
                    dve.tensor_tensor(s, s, h32[:, e % 2, m], ALU.mult).then_inc(c_u, 1)
                else:
                    go(dve.tensor_tensor(s, s, h32[:, e % 2, m], ALU.mult))
                    dve.tensor_tensor(s, s, su[:, 0, m], ALU.add).then_inc(c_u, 1)

            def u_low(cc, d, par):
                e = d if d < NEXP else NE - 1
                D = (NEXP + 1) * cc + d
                for m in range(KT):
                    dve.wait_ge(c_uh, 2 * D + m + 1)
                    dve.tensor_tensor(ul[:, (par + d) % 2, m], su[:, e % 2, m], uh[:, (par + d) % 2, m].bitcast(F32),
                                      ALU.subtract).then_inc(c_ul, 1)

            def residual(cc, par, first):
                if not first:
                    dve.wait_ge(x_stored, 16 * (NCH + cc))
                dve.wait_ge(c_down, (NEXP + 1) * (cc + 1))
                for m in range(KT):
                    dve.scalar_tensor_tensor(ysb[:, m], ps[:, 4 + m], bds[:, m:m + 1], xc[:, par, m], ALU.add, ALU.add
                                             ).then_inc(c_y, 1)

            def keep_mean_square(cc):
                dve.wait_ge(c_ms, cc + 1)
                dve.tensor_copy(rs, ps[:, 7]).then_inc(c_msread, 1)

            def new_x(cc, layer):
                dve.wait_ge(c_rs, cc + 1)
                for m in range(KT):
                    w = nw[:, layer, m:m + 1] if isinstance(layer, int) else \
                        nw.rearrange("p j k -> p (j k)")[:, bass.ds(layer * KT + m, 1)]
                    dve.scalar_tensor_tensor(ysb[:, m], ysb[:, m], w, rs, ALU.mult, ALU.mult).then_inc(c_xnew, 1)

            def lay(v, layer):
                return v[:, layer] if isinstance(layer, int) else \
                    v.rearrange("p j k -> p (j k)")[:, bass.ds(layer * NEXP, NEXP)]

            def route_a(cc):
                dve.wait_ge(c_logits, cc + 1)
                dve.tensor_copy(lgT, ps[0:32, 7]).then_inc(c_logits_read, 1)

            def route_b(cc, layer, part):
                if part == 0:
                    dve.wait_ge(c_logits_read, cc + 1)
                    go(dve.transpose(lgt.rearrange("p a b -> p (a b)"), lgT))
                    lg = lgt[:, :, 0:NEXP] if isinstance(layer, int) and layer == 0 else \
                        (lgt[:, :, NEXP:2 * NEXP] if isinstance(layer, int)
                         else lgt[:, :, bass.ds(layer * NEXP, NEXP)])
                    go(dve.tensor_tensor(gg, lg, lay(rb, layer).unsqueeze(1).broadcast_to((32, 16, NEXP)), ALU.add))
                    go(dve.tensor_tensor(biased, gg, lay(gb, layer).unsqueeze(1).broadcast_to((32, 16, NEXP)),
                                         ALU.add))
                elif part == 1:
                    go(dve.tensor_tensor(cmp, biased.unsqueeze(2).broadcast_to((32, 16, NEXP, NEXP)),
                                         biased.unsqueeze(3).broadcast_to((32, 16, NEXP, NEXP)), ALU.is_gt))
                    go(dve.tensor_tensor(cmp, cmp, upper.unsqueeze(1).broadcast_to((32, 16, NEXP, NEXP)), ALU.mult))
                    st.done(dve.tensor_reduce(r1, cmp, AX, ALU.add))
                    go(dve.tensor_reduce(r2, cmp.rearrange("p n e j -> p n j e"), AX, ALU.add))
                else:
                    go(dve.tensor_tensor(r1, r1, r2, ALU.subtract))
                    go(dve.tensor_tensor(sel, r1, thr.unsqueeze(1).broadcast_to((32, 16, NEXP)), ALU.is_lt))
                    st.done(dve.tensor_tensor(gg, gg, sel, ALU.mult))
                    go(dve.tensor_scalar(r1, sel, -NEG, NEG, ALU.mult, ALU.add))
                    go(dve.tensor_tensor(gg, gg, r1, ALU.add))
                    go(dve.tensor_reduce(rsum, gg, AX, ALU.max))
                    dve.tensor_tensor(gg, gg, rsum.unsqueeze(2).broadcast_to((32, 16, NEXP)), ALU.subtract
                                      ).then_inc(c_lg, 1)

            def route_c(cc, par):
                dve.wait_ge(c_re, cc + 1)
                go(dve.tensor_reduce(rsum, wgt, AX, ALU.add))
                go(dve.reciprocal(rsum, rsum))
                go(dve.tensor_tensor(wgt, wgt, rsum.unsqueeze(2).broadcast_to((32, 16, NEXP)), ALU.mult))
                go(dve.tensor_copy(whl[:, :, 0:NEXP], wgt))
                go(dve.tensor_tensor(whl[:, :, NEXP:2 * NEXP], wgt, whl[:, :, 0:NEXP].bitcast(F32), ALU.subtract))
                go(dve.transpose(lgT, whl[:, :, :].rearrange("p a b -> p (a b)").bitcast(F32)))
                dve.tensor_copy(wT[:, par], lgT).then_inc(c_wT, 1)

            def chunk(cc, par, first, last, layer_now, layer_next):
                for e in range(NE):
                    gated(cc, e, 0)
                    if e < NE - 1:
                        hidden_low(cc, e + 1)
                    elif not last:
                        hidden_low(cc + 1, 0)
                    gated(cc, e, 1)
                    if e == 6:
                        u_low(cc, 5, par)
                    elif e != 5:
                        u_low(cc, min(e, NEXP), par)
                    if not first:
                        if e == 0:
                            residual(cc - 1, 1 - par, False)
                        if e == 1:
                            keep_mean_square(cc - 1)
                        if e == 6:
                            new_x(cc - 1, layer_now)
                    if not last:
                        if e == 2:
                            route_a(cc + 1)
                        if e in (2, 3, 4):
                            route_b(cc + 1, layer_next, e - 2)
                        if e == 5:
                            split_x(cc + 1, 1 - par)
                        if e == 6:
                            route_c(cc + 1, 1 - par)

            split_x(0, 0)
            dve.wait_ge(ffn_w_ready, FFN_W_STEPS)
            route_a(0)
            for part in range(3):
                route_b(0, 0, part)
            route_c(0, 0)
            hidden_low(0, 0)
            total = LAYERS * NCH
            chunk(0, 0, True, False, 0, 0)
            with dve.Fori(0, total // 2 - 1) as i:
                st.enter(i, C_STEPS)
                chunk(2 * i + 1, 1, False, False, (2 * i) // NCH, (2 * i + 2) // NCH)
                chunk(2 * i + 2, 0, False, False, (2 * i + 1) // NCH, (2 * i + 3) // NCH)
                st.leave(total // 2 - 1)
            chunk(total - 1, 1, False, True, LAYERS - 1, None)
            residual(total - 1, 1, False)
            keep_mean_square(total - 1)
            new_x(total - 1, LAYERS - 1)

            def d_chunk(c, first):
                dve.wait_ge(d_in, 16 * (KVH + 1) * (c + 1))
                af = ain.rearrange("p k n -> p (k n)")
                a16 = ain.rearrange("p k (h d) -> p (k h) d", d=VD)
                go(dve.tensor_scalar(dsq, af, SQ_MAX, -SQ_MAX, ALU.min, ALU.max))
                go(dve.scalar_tensor_tensor(dsq, dsq, 2.0 ** -8, dsq, ALU.mult, ALU.mult))
                go(dve.tensor_reduce(dss, dsq.rearrange("p (n d) -> p n d", d=VD), AX, ALU.add))
                st.done(dve.tensor_scalar(dfin, dss, SQ_MAX * SQ_MAX * 2.0 ** -8, None, ALU.is_lt))
                dve.tensor_scalar(dss, dss, 2.0 ** -8 / VD, 1e-6 * 2.0 ** -16, ALU.mult, ALU.add
                                  ).then_inc(d_ss, 1)
                dve.wait_ge(d_sd, c + 1)
                go(dve.reciprocal(dsd, dsd))
                go(dve.scalar_tensor_tensor(dsd, dsd, 2.0 ** -8, dfin, ALU.mult, ALU.mult))
                dve.tensor_tensor(a16, a16, dsd.unsqueeze(2).broadcast_to((P, TB * 16, VD)), ALU.mult
                                  ).then_inc(d_an, 1)
                dve.wait_ge(d_proj, c + 1)
                if not first:
                    dve.wait_ge(d_back, c)
                for m in range(KT):
                    dve.wait_ge(d_silu, 2 * c + m + 1)
                    dve.tensor_tensor(sT[:, m], ps[:, 2 + m], sgT[:, m], ALU.mult).then_inc(d_s, 1)
                dve.wait_ge(d_back, c + 1)
                xf = xres.rearrange("p k n -> p (k n)")
                dve.tensor_tensor(xf[:, 0:C], xf[:, 0:C], ps[:, 4], ALU.add).then_inc(d_fin, 1)
                dve.tensor_tensor(xf[:, C:2 * C], xf[:, C:2 * C], ps[:, 5], ALU.add).then_inc(d_fin, 1)

            d_chunk(0, True)
            with dve.Fori(1, NCH) as c:
                st.enter(c - 1, D_STEPS)
                d_chunk(c, False)
                st.leave(NCH - 1)


_INS = ["L0_attn_x", "L0_attn_Wq", "L0_attn_Wk", "L0_attn_Wv", "L0_attn_Wo",
        "L0_attn_lambda_q1", "L0_attn_lambda_k1", "L0_attn_lambda_q2", "L0_attn_lambda_k2", "L0_attn_rms_w",
        "L0_ffn_router_W", "L0_ffn_router_b", "L0_ffn_gate_bias", "L0_ffn_exp_Wup", "L0_ffn_exp_bup",
        "L0_ffn_exp_Wg", "L0_ffn_exp_bg", "L0_ffn_exp_Wdown", "L0_ffn_exp_bdown", "L0_ffn_share_Wup",
        "L0_ffn_share_bup", "L0_ffn_share_Wg", "L0_ffn_share_bg", "L0_ffn_share_Wdown", "L0_ffn_share_bdown",
        "L0_ffn_norm_w"]


def shape_constants():
    inv = (1.0 / 10000.0 ** (np.arange(0, HD, 2, dtype=np.float32) / HD)).astype(np.float32)
    freqs = np.outer(np.arange(T, dtype=np.float32), inv).astype(np.float32)
    rows = np.arange(P)
    e = np.arange(NEXP)
    return {
        "rope_cos": np.ascontiguousarray(np.cos(freqs).T[rows // 32]).astype(np.float32),
        "rope_sin": np.ascontiguousarray(np.sin(freqs).T[rows // 32]).astype(np.float32),
        "rope_sign": np.where((rows // 16) % 2 == 0, 1.0, -1.0).astype(np.float32)[:, None],
        "upper": (e[None, :] > e[:, None]).astype(np.float32),
        "thr": (2.0 - e).astype(np.float32),
    }


def kernel(**inputs):
    import concourse.bacc as bacc
    from concourse.bass_utils import run_bass_kernel_spmd

    nc = bacc.Bacc("TRN2", target_bir_lowering=False, num_devices=1)
    arrays, aps = {}, {}
    for name, a in [(n, inputs[n]) for n in _INS] + list(shape_constants().items()):
        a = np.ascontiguousarray(a)
        arrays["in_" + name] = a
        aps[name] = nc.dram_tensor("in_" + name, a.shape, mybir.dt.from_np(a.dtype), kind="ExternalInput").ap()
    out = nc.dram_tensor("out_x", (B, T, E), F32, kind="ExternalOutput").ap()
    build(nc, aps, out)
    r = run_bass_kernel_spmd(nc, [arrays], core_ids=[0])
    return r.results[0]["out_x"]
```

```python
from contextlib import ExitStack
import math

import numpy as np

import concourse.bass as bass
from concourse import mybir

F32 = mybir.dt.float32
F32R = mybir.dt.float32r
BF16 = mybir.dt.bfloat16
ALU = mybir.AluOpType
ACT = mybir.ActivationFunctionType
AX = mybir.AxisListType.X

P = 128
B, T, E = 4, 1024, 256
N = B * T
KT = E // P
C = 512
TB = C // P
NCH = N // C
NQ, NK, KVH, HD = 32, 16, 8, 8
VD = 2 * HD
MAPS = NQ // KVH
UNITS = B * KVH
NEXP, NSH, LAYERS = 6, 2, 2
NE = NEXP + NSH
A_STEPS, B_STEPS, C_STEPS = 32, 10, 66
LAMBDA_INIT = 0.8 - 0.6 * math.exp(-0.3 * 12)
SCALE = HD ** -0.5
NEG = -1e30
SQ_MAX = 2.0 ** 64

ZROWS = 96
SROWS = ZROWS + 2

GROUPS = [(h, j) for h in range(2) for j in range(4 * (h + 1))]
JOBS = MAPS * len(GROUPS)
MAXJ = [(i, 0, m) for i in range(4) for m in range(MAPS)] + \
       [(i, p, m) for i in range(4, 8) for p in range(2) for m in range(MAPS)]
MAXA = 4 * MAPS
assert len(MAXJ) == JOBS
SRING = 3
LEAD = 43
PRING = 8
SHIFT_B_AT, OT_B_AT, OT_A_AT, SHIFT_A_AT = 9, 13, 25, 28
OT_EVAC_B_AT, OT_EVAC_A_AT = 4, 20
VALUES_AT = 3
FFN_SPLIT_AT, FFN_EXP_AT = 8, 44

W_UP, W_GATE, W_DOWN, NW = 0, NE, NE + NEXP + 1, NE + 2 * (NEXP + 1)


class Steps:

    def __init__(self, eng, sem):
        self.eng, self.sem, self.base, self.n = eng, sem, 0, 0

    def done(self, ins):
        self.n += 1
        ins.then_inc(self.sem, 1)

    def wait(self):
        self.eng.wait_ge(self.sem, self.base + self.n)

    def enter(self, turn, per):
        self.start = self.base + self.n
        self.base, self.n, self.per = self.start + turn * per, 0, per

    def leave(self, turns):
        assert self.n == self.per, (self.n, self.per)
        self.base, self.n = self.start + turns * self.per, 0


def build(nc, t, out):
    with ExitStack() as ctx:
        def sb(name, shape, dt=F32):
            return ctx.enter_context(nc.sbuf_tensor(name, shape, dt))

        def sem(name):
            return ctx.enter_context(nc.semaphore(name))

        def dram(name, shape, dt=F32):
            return nc.dram_tensor(name, shape, dt).ap()

        q_scr = dram("q_scr", (2, HD, UNITS, MAPS, T), F32R)
        k_scr = dram("k_scr", (HD, 2, UNITS, 2, T), F32R)
        v_scr = dram("v_scr", (B, KVH, T, VD))
        x_scr = dram("x_scr", (NCH, P, KT, C))
        a_scr = dram("a_scr", (2, P, TB, UNITS, 2 * VD))

        WH = sb("WH", [P, NW, 512], F32R)
        WL = sb("WL", [P, NW, 512], F32R)
        wstage = sb("wstage", [P, 2, 512])
        wq = sb("wq", [P, KT, 2, P])
        wk = sb("wk", [P, KT, 2, P])
        wv = sb("wv", [P, KT, P])
        wo = sb("wo", [P, KT, E])
        ident = sb("ident", [P, P])
        identb = sb("identb", [P, P], BF16)
        maskq = sb("maskq", [P, P], BF16)
        maskk = sb("maskk", [P, P], BF16)
        meanw = sb("meanw", [P, P])
        small = sb("small", [P, 512])
        rbuf = sb("rbuf", [P, 12288], F32R)
        fbuf = sb("fbuf", [P, 8704])
        wT = sb("wT", [32, 2, C], F32R)
        whl = sb("whl", [32, 16, 32], F32R)
        selw = sb("selw", [32, NEXP, P], F32R)
        bdr = sb("bdr", [32, 2, E], F32R)

        def carve(buf, sizes):
            views, at = [], 0
            for shape in sizes:
                n = int(np.prod(shape))
                v = buf[:, at:at + n]
                at += n
                names = "abcd"[:len(shape)]
                if len(shape) > 1:
                    v = v.rearrange(f"p ({' '.join(names)}) -> p {' '.join(names)}",
                                    **dict(zip(names, shape)))
                views.append(v)
            assert at <= buf.shape[1], (at, buf.shape)
            return views

        (lamv, lamp, lams, lame, lamneg, sgn, bup, bg, bds, nw, rmsw, mv, bst, rst, epsn) = carve(small, [
            (4, HD), (2, HD), (2,), (2,), (1,), (1,), (NE, KT), (NEXP + 1, KT), (KT,), (LAYERS, KT), (1,),
            (TB, 2), (TB, 6), (TB,), (1,)])
        qhl, khl = carve(rbuf, [(2, 2, 2, C), (2, 2, C)])
        xin, xst, cosT, sinT, rope0, rope1, ropeB = carve(fbuf, [
            (2, TB, E), (2, KT, C), (T,), (T,), (C,), (C,), (C,)])
        vst = wstage[:, :, :].rearrange("p a (k n) -> p a k n", k=TB)
        roped = (rope0, rope1, rope0)
        qst1, kst1, qst0, kst0 = carve(rbuf, [(2, MAPS, C), (2, T), (2, MAPS, C), (2, T)])
        qst, kst = (qst0, qst1), (kst0, kst1)
        probs, otsb, ot_e, attn_st = carve(fbuf, [(PRING, C), (C,), (16, VD), (2, TB, 2 * VD)])
        vu = fbuf[:, 8192:8704].rearrange("p (a k d) -> p a k d", a=2, k=8)
        mx = sb("mx", [P, 2, 2, 16])
        mparts = sb("mparts", [P, 2, 2, 16], F32R)
        mrows = sb("mrows", [32, 2, P], F32R)
        rec = sb("rec", [P, 16])
        uh, ul, _, xh, xl, hh, hl = carve(rbuf, [
            (2, KT, C), (2, KT, C), (2, KT, C), (2, KT, C), (2, KT, C), (KT, C), (KT, C)])
        h32, su, ysb, sq, rs, xc = carve(fbuf, [(2, KT, C), (2, KT, C), (KT, C), (KT, C), (C,), (2, KT, C)])
        rms_in = wstage[:, :, :].rearrange("p a n -> p (a n)")
        rms_sq = tuple(w[:, :, :, :].rearrange("p k a n -> p (k a n)") for w in (wq, wk))
        rms_sum, rms_fin, rms_exp, _ = carve(wv[:, :, :].rearrange("p k n -> p (k n)"), [(TB * E // VD,)] * 4)
        ain, aT, _, sT, sgT, _, xres = carve(fbuf, [
            (2, TB, E), (KT, C), (KT, C), (KT, C), (KT, C), (C,), (2, TB, E)])
        gT = ((wstage[:, 0], wstage[:, 1]), rms_sq)

        rt = sb("rt", [32, 2048])
        rw = sb("rw", [P, KT, 32])

        def carve32(sizes):
            views, at = [], 0
            for shape in sizes:
                n = int(np.prod(shape))
                v = rt[:, at:at + n]
                at += n
                names = "abcd"[:len(shape)]
                if len(shape) > 1:
                    v = v.rearrange(f"p ({' '.join(names)}) -> p {' '.join(names)}",
                                    **dict(zip(names, shape)))
                views.append(v)
            assert at <= 2048, at
            return views

        (rb, gb, upper, thr, lgt, gg, biased, cmp, r1, r2, sel, wgt, rsum, bdst) = carve32([
            (LAYERS, NEXP), (LAYERS, NEXP), (NEXP, NEXP), (NEXP,), (16, 32), (16, NEXP), (16, NEXP),
            (16, NEXP, NEXP), (16, NEXP), (16, NEXP), (16, NEXP), (16, NEXP), (16,), (E,)])
        lgT = cmp.rearrange("p a b c -> p (a b c)")[:, 0:C]

        ps = ctx.enter_context(nc.psum_tensor("ps", [P, 8, 512], F32))

        consts_in = sem("consts_in")
        wraw_in = sem("wraw_in")
        ident_ready = sem("ident_ready")
        consts_ready = sem("consts_ready")
        wproj_ready = sem("wproj_ready")
        dve_consts = sem("dve_consts")
        act_consts = sem("act_consts")
        dve_step = sem("dve_step")
        act_step = sem("act_step")
        pool_step = sem("pool_step")
        wstage_in = sem("wstage_in")
        ffn_w_ready = sem("ffn_w_ready")

        a_xin = [sem(f"a_xin{h}") for h in range(2)]
        a_stats, a_sd = sem("a_stats"), sem("a_sd")
        a_normed, a_transposed, a_xt = sem("a_normed"), sem("a_transposed"), sem("a_xt")
        a_proj_q, a_proj_k, a_proj_v = sem("a_proj_q"), sem("a_proj_k"), sem("a_proj_v")
        a_roped, a_high, a_split, a_vst = sem("a_roped"), sem("a_high"), sem("a_split"), sem("a_vst")
        a_qk_out = [sem(f"a_qk_out{h}") for h in range(2)]
        a_v_out = sem("a_v_out")

        b_zero = [sem(f"b_zero{p}") for p in range(2)]
        b_qk_in = [[sem(f"b_qk_in{p}{h}") for h in range(2)] for p in range(2)]
        b_v_in = [sem(f"b_v_in{p}") for p in range(2)]
        b_shift_in = [[sem(f"b_shift_in{p}{h}") for h in range(2)] for p in range(2)]
        b_scores, b_exp, b_pv = sem("b_scores"), sem("b_exp"), sem("b_pv")
        b_maxs, b_maxed = sem("b_maxs"), sem("b_maxed")
        b_mparts, b_mturned, b_mrows = sem("b_mparts"), sem("b_mturned"), sem("b_mrows")
        b_ot_out, b_ot_turned, b_ot_read, b_attn = (
            sem("b_ot_out"), sem("b_ot_turned"), sem("b_ot_read"), sem("b_attn"))
        b_attn_out = [sem(f"b_attn_out{h}") for h in range(2)]

        x_stored = sem("x_stored")
        c_xin = [sem(f"c_xin{h}") for h in range(2)]
        c_xh, c_xl, c_up, c_h32, c_hl = (
            sem("c_xh"), sem("c_xl"), sem("c_up"), sem("c_h32"), sem("c_hl"))
        c_gate, c_silu, c_wb, c_u = sem("c_gate"), sem("c_silu"), sem("c_wb"), sem("c_u")
        c_uh, c_ul, c_down, c_y, c_sq = sem("c_uh"), sem("c_ul"), sem("c_down"), sem("c_y"), sem("c_sq")
        c_ms, c_msread, c_ln, c_rs, c_xnew = sem("c_ms"), sem("c_msread"), sem("c_ln"), sem("c_rs"), sem("c_xnew")
        c_logits, c_logits_read, c_lg, c_re, c_wT = (
            sem("c_logits"), sem("c_logits_read"), sem("c_lg"), sem("c_re"), sem("c_wT"))

        d_ain, d_gin, d_xin = ([sem(f"{n}{h}") for h in range(2)] for n in ("d_ain", "d_gin", "d_xin"))
        rms_loaded, rms_stored = sem("rms_loaded"), sem("rms_stored")
        d_turned, d_aT = sem("d_turned"), sem("d_aT")
        d_proj, d_silu, d_s, d_back, d_fin = (
            sem("d_proj"), sem("d_silu"), sem("d_s"), sem("d_back"), sem("d_fin"))
        d_out = [sem(f"d_out{h}") for h in range(2)]

        block = ctx.enter_context(nc.Block())
        N_CONSTS = 23
        FFN_W_STEPS = 2 * NW + 2

        def clear_stacks(eng, st, par):
            st.done(eng.memset(qst[par].rearrange("p a m t -> p (a m t)").bitcast(F32), 0.0))
            st.done(eng.memset(kst[par].rearrange("p s t -> p (s t)").bitcast(F32), 0.0))
            st.wait()
            eng.memset(kst[par][ZROWS:P].rearrange("p s t -> p (s t)").bitcast(F32), 1.0).then_inc(b_zero[par], 1)

        @block.sync
        def _(sp):
            sp.dma_start(wstage[:, 0, :].rearrange("p (k n) -> p k n", k=KT),
                         t["L0_attn_Wq"].rearrange("(k p) n -> p k n", p=P)).then_inc(wraw_in, 16)
            sp.dma_start(wstage[:, 1, 0:KT * P].rearrange("p (k n) -> p k n", k=KT),
                         t["L0_attn_Wk"].rearrange("(k p) n -> p k n", p=P)).then_inc(wraw_in, 16)
            x_v = t["L0_attn_x"].rearrange("b (h k p) e -> h b p k e", h=2, p=P)
            for h in range(2):
                sp.dma_start(xin[:, h], x_v[h, 0]).then_inc(a_xin[h], 16)
            n = 0

            def load(dst, src):
                nonlocal n
                n += 1
                sp.dma_start(dst, src).then_inc(consts_in, 16)

            load(wv[:, :, :], t["L0_attn_Wv"].rearrange("(k p) n -> p k n", p=P))
            load(cosT, t["rope_cos"])
            load(sinT, t["rope_sin"])
            load(sgn, t["rope_sign"])
            load(wo[:, :, :], t["L0_attn_Wo"].rearrange("(k p) n -> p k n", p=P))
            for i, name in enumerate(("q1", "k1", "q2", "k2")):
                load(lamv[:, i], t["L0_attn_lambda_" + name].partition_broadcast(P))
            with nc.allow_non_contiguous_dma("small bias tables"):
                for k in range(KT):
                    load(bup[:, 0:NEXP, k], t["L0_ffn_exp_bup"][:, k * P:(k + 1) * P].rearrange("e p -> p e"))
                    load(bg[:, 0:NEXP, k], t["L0_ffn_exp_bg"][:, k * P:(k + 1) * P].rearrange("e p -> p e"))
                    load(nw[:, :, k], t["L0_ffn_norm_w"][:, k * P:(k + 1) * P].rearrange("j p -> p j"))
                load(bup[:, NEXP:NE, :].rearrange("p e k -> p (e k)"),
                     t["L0_ffn_share_bup"].rearrange("(e p) -> p e", p=P))
                load(bg[:, NEXP, :], t["L0_ffn_share_bg"].rearrange("(k p) -> p k", p=P))
                load(bds, t["L0_ffn_share_bdown"].rearrange("(k p) -> p k", p=P))
                load(rmsw, t["L0_attn_rms_w"].partition_broadcast(P // VD).unsqueeze(2))
            load(rb, t["L0_ffn_router_b"].partition_broadcast(32))
            load(gb, t["L0_ffn_gate_bias"].partition_broadcast(32))
            load(upper, t["upper"].partition_broadcast(32))
            load(thr, t["thr"].partition_broadcast(32))
            assert n == N_CONSTS, n

            def stores(c, h):
                b, t0 = c // 2, C * h
                if not (isinstance(c, int) and c == 0):
                    sp.wait_ge(x_stored, 16 * c)
                sp.wait_ge(a_xt, KT * (c + 1))
                sp.dma_start(x_scr[c], xst[:, h]).then_inc(x_stored, 16)
                sp.wait_ge(a_split, 3 * (c + 1))
                for a in range(2):
                    for part in range(2):
                        d = q_scr[part].rearrange("(d a) (b g) m t -> a d b (g m) t", a=2, b=B)
                        sp.dma_start(d[a, :, b, :, t0:t0 + C].bitcast(F32),
                                     qhl[:, h, a, part].bitcast(F32)).then_inc(a_qk_out[h], 16)
                for part in range(2):
                    d = k_scr[:, part].rearrange("d (b g) s t -> d b (g s) t", b=B)
                    sp.dma_start(d[:, b, :, t0:t0 + C].bitcast(F32),
                                 khl[:, h, part].bitcast(F32)).then_inc(a_qk_out[h], 16)
                if not (isinstance(c, int) and c == 0):
                    sp.wait_ge(a_v_out, 16 * TB * c)
                sp.wait_ge(a_vst, c + 1)
                for k in range(TB):
                    d = v_scr[b, :, t0 + k * P:t0 + (k + 1) * P, :].rearrange("g p d -> p g d")
                    sp.dma_start(d, vst[:, h, k].rearrange("p (g d) -> p g d", g=KVH)).then_inc(a_v_out, 16)

            def load_qk(u, par):
                for h in range(2):
                    ts = slice(C * h, C * (h + 1))
                    for r in range(2):
                        sp.dma_start(qst[par][r:32:2, h].bitcast(F32),
                                     q_scr[:, :, u, :, ts].rearrange("a d m t -> (a d) m t").bitcast(F32)
                                     ).then_inc(b_qk_in[par][h], 16)
                        sp.dma_start(kst[par][16 * r:16 * r + 16, :, ts].bitcast(F32),
                                     k_scr[:, :, u, :, ts].rearrange("d a s t -> (d a) s t").bitcast(F32)
                                     ).then_inc(b_qk_in[par][h], 16)

            def load_v(u, par):
                vv = v_scr.rearrange("b g (k p) d -> (b g) p k d", p=P)
                sp.dma_start(vu[:, par, :, 0:VD], vv[u]).then_inc(b_v_in[par], 16)

            stores(0, 0)
            stores(1, 1)
            for h in range(2):
                sp.wait_ge(a_qk_out[h], 16 * 6)
            sp.wait_ge(a_v_out, 16 * TB * 2)
            sp.wait_ge(b_zero[0], 1)
            sp.wait_ge(consts_ready, 8)
            load_qk(0, 0)
            load_v(0, 0)
            with sp.Fori(1, B) as b:
                stores(2 * b, 0)
                stores(2 * b + 1, 1)

            for h in range(2):
                sp.wait_ge(a_qk_out[h], 16 * 6 * B)
            sp.wait_ge(a_v_out, 16 * TB * NCH)
            sp.wait_ge(b_zero[1], 1)

            def store_shift(u, par, h):
                sp.wait_ge(b_mrows, 2 * u + h + 1)
                sp.dma_start(qst[par][ZROWS:SROWS, h].rearrange("r m t -> r (m t)").bitcast(F32),
                             mrows[:, h].bitcast(F32)).then_inc(b_shift_in[par][h], 16)

            def store_attn(u, h):
                sp.wait_ge(b_attn, 2 * u + h + 1)
                sp.dma_start(a_scr[h, :, :, u],
                             attn_st[:, h]).then_inc(b_attn_out[h], 16)

            def unit(u, par, first, last):
                if not last:
                    if not first:
                        sp.wait_ge(b_scores, JOBS * u)
                    load_qk(u + 1, 1 - par)
                    if not first:
                        sp.wait_ge(b_pv, JOBS * u)
                    load_v(u + 1, 1 - par)
                store_shift(u, par, 1)
                if not first:
                    store_attn(u - 1, 1)
                store_attn(u, 0)
                if not last:
                    store_shift(u + 1, 1 - par, 0)

            def load_state(c, x, par):
                sp.dma_start(xc[:, par], x_scr[x]).then_inc(c_xin[par], 16)

            store_shift(0, 0, 0)
            unit(0, 0, True, False)
            with sp.Fori(0, UNITS // 2 - 1) as i:
                unit(2 * i + 1, 1, False, False)
                unit(2 * i + 2, 0, False, False)
            sp.wait_ge(x_stored, 16 * NCH)
            load_state(0, 0, 0)
            unit(UNITS - 1, 1, False, True)
            store_attn(UNITS - 1, 1)

            total = LAYERS * NCH
            sp.wait_ge(b_exp, JOBS * UNITS)
            sp.wait_ge(b_pv, JOBS * UNITS)
            sp.wait_ge(b_ot_turned, 2 * UNITS)
            for h in range(2):
                sp.wait_ge(b_attn_out[h], 16 * UNITS)

            def c_turn(cc, par):
                sp.wait_ge(x_stored, 16 * (NCH + cc))
                sp.wait_ge(c_y, 2 * cc + 2)
                load_state(cc + 2, (cc + 2) % NCH, par)
                sp.wait_ge(c_xnew, 2 * cc + 2)
                sp.dma_start(x_scr[cc % NCH], ysb).then_inc(x_stored, 16)

            load_state(1, 1, 1)
            with sp.Fori(0, total // 2 - 1) as i:
                c_turn(2 * i, 0)
                c_turn(2 * i + 1, 1)
            sp.wait_ge(c_xnew, 2 * total - 2)
            sp.dma_start(x_scr[(total - 2) % NCH], ysb).then_inc(x_stored, 16)

            xr = t["L0_attn_x"].rearrange("b (h k p) e -> (b h) p k e", h=2, p=P)
            ov = out.rearrange("b (h k p) e -> (b h) p k e", h=2, p=P)

            def load_attn(c, par):
                sp.dma_start(ain[:, par], a_scr.rearrange("h p k (b g) d -> h b p k (g d)", b=B)[par, c // 2]
                             ).then_inc(d_ain[par], 16)

            def load_gate(c, par):
                for k in range(KT):
                    sp.dma_start(gT[par][k], x_scr[c][:, k]).then_inc(d_gin[par], 16)

            def load_x(c, par):
                sp.dma_start(xres[:, par], xr[c]).then_inc(d_xin[par], 16)

            def d_step(c, par, more_attn=True, more=True, last=False, first=False):
                if more_attn:
                    sp.wait_ge(d_turned, c + 3)
                    load_attn(c + 4, par)
                if more:
                    sp.wait_ge(d_silu, KT * (c + 1))
                    load_gate(c + 2, par)
                sp.wait_ge(d_fin, 2 * c + 2)
                sp.dma_start(ov[c], xres[:, par]).then_inc(d_out[par], 16)
                if not first and not last:
                    sp.wait_ge(d_out[1 - par], 16 * ((c + 1) // 2))
                    load_x(c + 1, 1 - par)

            sp.wait_ge(rms_stored, 16 * NCH)
            sp.wait_ge(c_y, 2 * total - 2)
            load_x(0, 0)
            sp.wait_ge(x_stored, 16 * (NCH + total - 1))
            for c in range(2):
                load_gate(c, c)
            sp.wait_ge(c_u, 2 * NE * total)
            for c in range(2):
                load_attn(c, c)
            sp.wait_ge(c_y, 2 * total)
            load_x(1, 1)
            sp.wait_ge(c_xnew, 2 * total)
            sp.dma_start(x_scr[(total - 1) % NCH], ysb).then_inc(x_stored, 16)
            for c in range(2, 4):
                sp.wait_ge(d_turned, c - 1)
                load_attn(c, c % 2)
            sp.wait_ge(x_stored, 16 * (NCH + total))
            d_step(0, 0, first=True)
            d_step(1, 1)
            for c in range(2, NCH):
                d_step(c, c % 2, c + 4 < NCH, c + 2 < NCH, c == NCH - 1)
            for par in range(2):
                sp.wait_ge(d_out[par], 16 * NCH // 2)

        @block.gpsimd
        def _(pool):
            st = Steps(pool, pool_step)
            st.done(pool.memset(ident[:, :], 0.0))
            st.wait()
            pool.affine_select(out=ident[:, :], in_=ident[:, :], pattern=[[-1, P]], compare_op=ALU.not_equal,
                               fill=1.0, base=0, channel_multiplier=1).then_inc(ident_ready, 1)
            pool.wait_ge(wraw_in, 32)
            for k in range(KT):
                raw = wstage[:, 0, k * E:(k + 1) * E].rearrange("p (h a d) -> p a d h", a=2, d=4)
                for a in range(2):
                    pool.tensor_copy(wq[:, k, a].rearrange("p (d h) -> p d h", d=4), raw[:, a]
                                     ).then_inc(wproj_ready, 1)
                raw = wstage[:, 1, k * P:(k + 1) * P].rearrange("p (h a d) -> p a d h", a=2, d=4)
                for s in range(2):
                    dst = wk[:, k, s].rearrange("p (d a h) -> p a d h", d=4, a=2)
                    for a in range(2):
                        pool.tensor_copy(dst[:, a], raw[:, a ^ s]).then_inc(wproj_ready, 1)
            st.done(pool.memset(identb[:, :], 0.0))
            st.done(pool.memset(maskq[:, :], 0.0))
            st.done(pool.memset(maskk[:, :], 0.0))
            st.done(pool.memset(selw[:, :, :].bitcast(F32), 0.0))
            pool.memset(meanw[:, :], 1.0 / E).then_inc(consts_ready, 1)
            pool.memset(rw[:, :, :], 0.0).then_inc(consts_ready, 1)
            pool.memset(whl[:, :, :].bitcast(F32), 0.0).then_inc(consts_ready, 1)
            pool.memset(bdr[:, :, :].bitcast(F32), 0.0).then_inc(consts_ready, 1)
            st.done(pool.memset(vu[:, :, :, :], 0.0))
            st.wait()
            pool.affine_select(out=identb[:, :], in_=identb[:, :], pattern=[[-1, P]], compare_op=ALU.not_equal,
                               fill=1.0, base=0, channel_multiplier=1).then_inc(consts_ready, 1)
            pool.affine_select(out=maskq[:, :], in_=maskq[:, :], pattern=[[-1, P]], compare_op=ALU.is_ge,
                               fill=NEG, base=0, channel_multiplier=1).then_inc(consts_ready, 1)
            pool.affine_select(out=maskk[:, :], in_=maskk[:, :], pattern=[[1, P]], compare_op=ALU.is_ge,
                               fill=NEG, base=0, channel_multiplier=-1).then_inc(consts_ready, 1)
            for off in (0, NEXP):
                st.done(pool.affine_select(out=selw[:, :, :], in_=selw[:, :, :].bitcast(F32),
                                           pattern=[[-1, NEXP], [0, P]], compare_op=ALU.not_equal,
                                           fill=1.0, base=-off, channel_multiplier=1))
                st.wait()
            pool.memset(vu[:, :, :, VD:VD + 1], 1.0).then_inc(consts_ready, 1)
            for h in range(2):
                pool.wait_ge(a_qk_out[h], 16 * 6 * B)
            pool.wait_ge(a_v_out, 16 * TB * NCH)
            clear_stacks(pool, st, 1)
            pool.wait_ge(b_zero[1], 1)

            up = t["L0_ffn_exp_Wup"].rearrange("e (k p) n -> e p k n", p=P)
            gate = t["L0_ffn_exp_Wg"].rearrange("e (k p) n -> e p k n", p=P)
            down = t["L0_ffn_exp_Wdown"].rearrange("e (k p) n -> e p k n", p=P)
            pool.wait_ge(wproj_ready, 12)

            def split(i, turn, slot, src, w, first):
                dst = wstage[:, slot].rearrange("p (k n) -> p k n", k=KT)
                pool.dma_start(dst, src).then_inc(wstage_in, 16)
                pool.wait_ge(wstage_in, 16 * (turn + 1))
                pool.tensor_copy(WH[:, w], wstage[:, slot]).then_inc(ffn_w_ready, 1)
                pool.wait_ge(ffn_w_ready, 2 * turn + 1)
                pool.tensor_tensor(WL[:, w], wstage[:, slot], WH[:, w].bitcast(F32), ALU.subtract
                                   ).then_inc(ffn_w_ready, 1)
                pool.wait_ge(ffn_w_ready, 2 * turn + 2)

            for e in range(NEXP):
                for j, (m, w0) in enumerate(((up, W_UP), (gate, W_GATE), (down, W_DOWN))):
                    n = 3 * e + j
                    split(e, n, n % 2, m[e], w0 + e, n < 2)
            share = [(t["L0_ffn_share_Wup"][:, E * s:E * (s + 1)], W_UP + NEXP + s) for s in range(NSH)]
            share += [(t["L0_ffn_share_Wg"], W_GATE + NEXP), (t["L0_ffn_share_Wdown"], W_DOWN + NEXP)]
            for j, (m, w) in enumerate(share):
                split(0, 3 * NEXP + j, j % 2, m.rearrange("(k p) n -> p k n", p=P), w, False)
            with nc.allow_non_contiguous_dma("router weights"):
                pool.wait_ge(consts_ready, 8)
                for j in range(LAYERS):
                    pool.dma_start(rw[:, :, NEXP * j:NEXP * (j + 1)],
                                   t["L0_ffn_router_W"][j].rearrange("(k p) e -> p k e", p=P)).then_inc(wstage_in, 16)
            pool.dma_start(bdst[0:NEXP], t["L0_ffn_exp_bdown"]).then_inc(wstage_in, 16)
            pool.dma_start(bdst[NEXP:2 * NEXP], t["L0_ffn_exp_bdown"]).then_inc(wstage_in, 16)
            pool.wait_ge(wstage_in, 16 * (NW + 4))
            pool.tensor_copy(bdr[0:2 * NEXP, 0], bdst[0:2 * NEXP]).then_inc(ffn_w_ready, 1)
            pool.wait_ge(ffn_w_ready, FFN_W_STEPS - 1)
            pool.tensor_tensor(bdr[0:2 * NEXP, 1], bdst[0:2 * NEXP], bdr[0:2 * NEXP, 0].bitcast(F32),
                               ALU.subtract).then_inc(ffn_w_ready, 1)
            pool.wait_ge(ffn_w_ready, FFN_W_STEPS)

            for h in range(2):
                pool.wait_ge(b_attn_out[h], 16 * UNITS)
            attn = a_scr.rearrange("h p k (b g) d -> h b p k (g d)", b=B)
            rms_v = rms_in.rearrange("p (k n) -> p k n", k=TB)

            def step(ins):
                st.done(ins)
                st.wait()

            def load_rms(b, h):
                pool.dma_start(rms_v, attn[h, b]).then_inc(rms_loaded, 16)

            def rms_chunk(b, h):
                c = 2 * b + h
                pool.wait_ge(rms_loaded, 16 * (c + 1))
                for i, sq_i in enumerate(rms_sq):
                    step(pool.tensor_scalar(sq_i, rms_in[:, C * i:C * (i + 1)], 2.0 ** -4, SQ_MAX * 2.0 ** -4,
                                            ALU.mult, ALU.min))
                    step(pool.tensor_scalar(sq_i, sq_i, -SQ_MAX * 2.0 ** -4, None, ALU.max))
                    step(pool.tensor_tensor(sq_i, sq_i, sq_i, ALU.mult))
                    v = sq_i.rearrange("p (n d) -> p n d", d=VD)
                    for w in (8, 4, 2):
                        step(pool.tensor_tensor(v[:, :, 0:w], v[:, :, 0:w], v[:, :, w:2 * w], ALU.add))
                    step(pool.tensor_tensor(rms_sum[:, i * C // VD:(i + 1) * C // VD], v[:, :, 0], v[:, :, 1], ALU.add))
                step(pool.tensor_scalar(rms_fin, rms_sum, SQ_MAX * SQ_MAX * 2.0 ** -8, 2.0 ** -8, ALU.is_lt, ALU.mult))
                step(pool.tensor_scalar(rms_sum, rms_sum, 2.0 ** -8 / VD, 1e-6 * 2.0 ** -16, ALU.mult, ALU.add))
                step(pool.tensor_tensor(rms_sum, rms_sum, rms_exp, ALU.pow))
                step(pool.tensor_tensor(rms_sum, rms_sum, rms_fin, ALU.mult))
                a = rms_in.rearrange("p (n d) -> p n d", d=VD)
                step(pool.tensor_tensor(a, a, rms_sum.unsqueeze(2).broadcast_to((P, TB * E // VD, VD)), ALU.mult))
                pool.dma_start(attn[h, b], rms_v).then_inc(rms_stored, 16)
                pool.wait_ge(rms_stored, 16 * (c + 1))

            step(pool.memset(rms_exp, -0.5))
            for c in range(NCH):
                load_rms(c // 2, c % 2)
                rms_chunk(c // 2, c % 2)

        @block.tensor
        def _(pe):
            def turn_x(c, h):
                pe.wait_ge(a_normed, TB * (c + 1))
                if not (isinstance(c, int) and c == 0):
                    pe.wait_ge(a_xt, KT * c)
                for m in range(KT):
                    for k in range(TB):
                        last = pe.transpose(ps[:, m, k * P:(k + 1) * P], xin[:, h, k, m * P:(m + 1) * P], ident[:, :])
                last.then_inc(a_transposed, 1)

            def project(c, h, first=False):
                pe.wait_ge(a_xt, KT * (c + 1))
                if not first:
                    pe.wait_ge(a_roped, 3 * c - 1)
                for a in range(2):
                    for k in range(KT):
                        last = pe.matmul(ps[:, 2 + a, :], wq[:, k, a], xst[:, h, k],
                                         start=(k == 0), stop=(k == KT - 1))
                last.then_inc(a_proj_q, 1)
                if not first:
                    pe.wait_ge(a_roped, 3 * c)
                for s in range(2):
                    for k in range(KT):
                        last = pe.matmul(ps[:, 4 + s, :], wk[:, k, s], xst[:, h, k],
                                         start=(k == 0), stop=(k == KT - 1))
                last.then_inc(a_proj_k, 1)
                if not first:
                    pe.wait_ge(a_vst, c)
                for tb in range(TB):
                    for k in range(KT):
                        last = pe.matmul(ps[:, 6, tb * P:(tb + 1) * P], xst[:, h, k, tb * P:(tb + 1) * P], wv[:, k],
                                         start=(k == 0), stop=(k == KT - 1))
                last.then_inc(a_proj_v, 1)

            pe.wait_ge(ident_ready, 1)
            turn_x(0, 0)
            pe.wait_ge(wproj_ready, 12)
            pe.wait_ge(consts_in, 16 * N_CONSTS)
            project(0, 0, True)
            turn_x(1, 1)
            project(1, 1)
            turn_x(2, 0)
            with pe.Fori(1, B - 1) as b:
                project(2 * b, 0)
                turn_x(2 * b + 1, 1)
                project(2 * b + 1, 1)
                turn_x(2 * b + 2, 0)
            project(NCH - 2, 0)
            turn_x(NCH - 1, 1)
            project(NCH - 1, 1)

            pe.wait_ge(consts_ready, 8)
            pe.wait_ge(a_roped, 3 * NCH)
            pe.wait_ge(a_vst, NCH)
            pe.wait_ge(a_xt, KT * NCH)
            ST, MX, OT, TR = 0, SRING, 6, 7

            def max_matmul(u, par, s, first=False):
                i, piece, m = MAXJ[s]
                if s == 0:
                    pe.wait_ge(b_qk_in[par][0], 64 * (u // 2 + 1))
                if s == MAXA:
                    pe.wait_ge(b_qk_in[par][1], 64 * (u // 2 + 1))
                if not (first and s < SRING):
                    pe.wait_ge(b_maxed, JOBS * u + s + 1 - SRING)
                width = min(512, P * (i + 1) - 512 * piece)
                o = ps[:, MX + s % SRING, 0:width]
                diag = piece == i // 4
                ins = pe.matmul(o, qst[par][0:ZROWS, i // 4, m, P * (i % 4):P * (i % 4 + 1)],
                                kst[par][0:ZROWS, m % 2, 512 * piece:512 * piece + width],
                                start=True, stop=not diag)
                if diag:
                    ins = pe.matmul(o[:, width - P:width], identb[:, :], maskq[:, :], start=False, stop=True)
                ins.then_inc(b_maxs, 1)

            def scores(u, par, s, first):
                (h, j), m = GROUPS[s // MAPS], s % MAPS
                if s in (0, MAPS * 4):
                    pe.wait_ge(b_shift_in[par][h], 16 * (u // 2 + 1))
                if not (first and s < SRING):
                    pe.wait_ge(b_exp, JOBS * u + s + 1 - SRING)
                t0 = max(0, P * j - C * h)
                o = ps[:, ST + s % SRING, t0:C]
                diag = P * j >= C * h
                ins = pe.matmul(o, kst[par][0:SROWS, m % 2, P * j:P * (j + 1)], qst[par][0:SROWS, h, m, t0:C],
                                start=True, stop=not diag)
                if diag:
                    ins = pe.matmul(o[:, 0:P], identb[:, :], maskk[:, :], start=False, stop=True)
                ins.then_inc(b_scores, 1)

            def values(u, par, s, first):
                (h, j), m = GROUPS[s // MAPS], s % MAPS
                if s == 0:
                    pe.wait_ge(b_v_in[par], 16 * (u // 2 + 1))
                if s in (0, MAPS * 4) and not (first and s == 0):
                    pe.wait_ge(b_ot_out, 2 * u + h)
                pe.wait_ge(b_exp, JOBS * u + s + 1)
                t0 = max(0, P * j - C * h)
                pe.matmul(ps[32 * m:32 * m + 32, OT, t0:C], vu[:, par, j, :], probs[:, s % PRING, t0:C],
                          start=(j == 0), stop=(j == 4 * h + 3)).then_inc(b_pv, 1)

            def turn_shift(u, h):
                pe.wait_ge(b_mparts, 2 * (2 * u + h) + 2)
                pe.transpose(ps[0:32, TR, 0:P], mparts[:, h].rearrange("p a n -> p (a n)").bitcast(F32),
                             ident[:, :]).then_inc(b_mturned, 1)

            def turn_ot(u, h):
                pe.wait_ge(b_ot_out, 2 * u + h + 1)
                for k in range(TB):
                    ins = pe.transpose(ps[:, TR, k * P:(k + 1) * P], otsb[:, k * P:(k + 1) * P], ident[:, :])
                ins.then_inc(b_ot_turned, 1)

            def unit(u, par, first, last):
                for s in range(JOBS):
                    scores(u, par, s, first)
                    if s < JOBS - LEAD:
                        max_matmul(u, par, s + LEAD)
                    elif not last:
                        max_matmul(u + 1, 1 - par, s + LEAD - JOBS)
                    if s % MAPS == VALUES_AT:
                        for m in range(MAPS):
                            if s >= MAPS:
                                values(u, par, s - VALUES_AT - MAPS + m, first)
                            elif not first:
                                values(u - 1, 1 - par, JOBS - MAPS + m, False)
                    if s == SHIFT_B_AT:
                        pe.wait_ge(b_mrows, 2 * u + 1)
                        turn_shift(u, 1)
                    if s == OT_B_AT and not first:
                        pe.wait_ge(b_mrows, 2 * u + 2)
                        turn_ot(u - 1, 1)
                    if s == OT_A_AT:
                        if first:
                            pe.wait_ge(b_mrows, 2)
                        else:
                            pe.wait_ge(b_ot_read, 2 * u)
                        turn_ot(u, 0)
                    if s == SHIFT_A_AT and not last:
                        pe.wait_ge(b_ot_read, 2 * u + 1)
                        turn_shift(u + 1, 0)
                    if s == SHIFT_A_AT and last:
                        pe.wait_ge(ffn_w_ready, FFN_W_STEPS)
                        pe.wait_ge(b_ot_read, 2 * u + 1)
                        route(0, 0)

            HB, ZB, YB, WB, LB = 0, 2, 4, 6, 7
            def product(o, w, m, hi, lo, start, stop):
                n = 0
                for k in range(KT):
                    cols = slice(E * k + P * m, E * k + P * (m + 1))
                    for ww, xx in ((WH, hi), (WL, hi), (WH, lo)):
                        ins = pe.matmul(o, ww[:, w, cols], xx[:, k], start=(start and n == 0),
                                        stop=(stop and n == 3 * KT - 1))
                        n += 1
                return ins

            def up(cc, e, par, first=False):
                G = NE * cc + e
                if e == 0:
                    pe.wait_ge(c_xl, KT * (cc + 1))
                for m in range(KT):
                    if not first:
                        pe.wait_ge(c_h32, 2 * G - 1 + m)
                    product(ps[:, HB + m], W_UP + e, m, xh[:, par], xl[:, par], True, True).then_inc(c_up, 1)

            def gate(cc, e, first=False):
                G = NE * cc + e
                pe.wait_ge(c_hl, 2 * G + 2)
                for m in range(KT):
                    if not first:
                        pe.wait_ge(c_silu, 2 * G - 2 + m + 1)
                    product(ps[:, ZB + m], W_GATE + min(e, NEXP), m, hh, hl, True, True).then_inc(c_gate, 1)

            def down_bias(cc, par, first=False):
                if not first:
                    pe.wait_ge(c_y, 2 * cc)
                for m in range(KT):
                    for part in range(2):
                        pe.matmul(ps[:, YB + m], bdr[:, part, P * m:P * (m + 1)], wT[:, par],
                                  start=(part == 0), stop=False)

            def down(cc, d, par):
                D = (NEXP + 1) * cc + d
                dp = (par + d) % 2
                pe.wait_ge(c_ul, 2 * D + 2)
                for m in range(KT):
                    ins = product(ps[:, YB + m], W_DOWN + d, m, uh[:, dp], ul[:, dp], False, d == NEXP)
                ins.then_inc(c_down, 1)

            def expert_weight(cc, e, par, first=False):
                if e == 0:
                    pe.wait_ge(c_wT, cc + 1)
                if not first:
                    pe.wait_ge(c_u, 2 * (NE * cc + (e if e else -1)))
                pe.matmul(ps[:, WB], selw[:, e], wT[:, par], start=True, stop=True).then_inc(c_wb, 1)

            def route(cc, par):
                pe.wait_ge(c_xin[par], 16 * (cc // 2 + 1))
                for k in range(KT):
                    ins = pe.matmul(ps[0:32, LB, :], rw[:, k, :], xc[:, par, k], start=(k == 0), stop=(k == KT - 1))
                ins.then_inc(c_logits, 1)

            def mean_square(cc):
                pe.wait_ge(c_sq, 2 * cc + 2)
                for m in range(KT):
                    ins = pe.matmul(ps[:, LB], meanw[:, :], sq[:, m], start=(m == 0), stop=(m == KT - 1))
                ins.then_inc(c_ms, 1)

            def chunk(cc, par, first, last):
                for e in range(NE):
                    if e < NE - 1:
                        up(cc, e + 1, par)
                    elif not last:
                        up(cc + 1, 0, 1 - par)
                    if e == 0 and not first:
                        down(cc - 1, NEXP, 1 - par)
                    if e == 1:
                        down_bias(cc, par, first)
                        if not first:
                            pe.wait_ge(c_logits_read, cc + 1)
                            mean_square(cc - 1)
                    if e > 1:
                        down(cc, e - 2, par)
                    if e < NE - 1:
                        gate(cc, e + 1)
                    elif not last:
                        gate(cc + 1, 0)
                    if e + 1 < NEXP:
                        expert_weight(cc, e + 1, par)
                    elif e == NE - 1 and not last:
                        expert_weight(cc + 1, 0, 1 - par)
                    if e == 2 and not last:
                        if not first:
                            pe.wait_ge(c_msread, cc)
                        route(cc + 1, 1 - par)

            for s in range(LEAD):
                max_matmul(0, 0, s, True)
                if s == MAXA + 4:
                    turn_shift(0, 0)
            unit(0, 0, True, False)
            with pe.Fori(0, UNITS // 2 - 1) as i:
                unit(2 * i + 1, 1, False, False)
                unit(2 * i + 2, 0, False, False)
            unit(UNITS - 1, 1, False, True)
            for s in range(JOBS - MAPS, JOBS):
                values(UNITS - 1, 1, s, False)
            pe.wait_ge(c_logits_read, 1)
            turn_ot(UNITS - 1, 1)

            pe.wait_ge(b_exp, JOBS * UNITS)
            pe.wait_ge(b_maxed, JOBS * UNITS)
            up(0, 0, 0, True)
            gate(0, 0, True)
            pe.wait_ge(b_ot_read, 2 * UNITS)
            expert_weight(0, 0, 0, True)
            chunk(0, 0, True, False)
            total = LAYERS * NCH
            with pe.Fori(0, total // 2 - 1) as i:
                chunk(2 * i + 1, 1, False, False)
                chunk(2 * i + 2, 0, False, False)
            chunk(total - 1, 1, False, True)
            down(total - 1, NEXP, 1)
            mean_square(total - 1)

            pe.wait_ge(c_y, 2 * total)

            def turn(c, par, first=False):
                pe.wait_ge(d_ain[par], 16 * (c // 2 + 1))
                if not first:
                    pe.wait_ge(d_aT, 2 * c)
                for m in range(KT):
                    for k in range(TB):
                        last = pe.transpose(ps[:, m, k * P:(k + 1) * P], ain[:, par, k, m * P:(m + 1) * P], ident[:, :])
                last.then_inc(d_turned, 1)

            def project(c, par, first=False):
                pe.wait_ge(d_aT, 2 * c + 2)
                if not first:
                    pe.wait_ge(d_s, 2 * c - 2)
                for m in range(KT):
                    for k in range(KT):
                        last = pe.matmul(ps[:, 2 + 4 * par + m], wo[:, k, m * P:(m + 1) * P], aT[:, k],
                                         start=(k == 0), stop=(k == KT - 1))
                last.then_inc(d_proj, 1)

            def turn_back(c, first=False):
                pe.wait_ge(d_s, 2 * c + 2)
                if not first:
                    pe.wait_ge(d_fin, 2 * c)
                for k in range(TB):
                    for m in range(KT):
                        last = pe.transpose(ps[:, 4 + k // 2, (k % 2) * E + m * P:(k % 2) * E + (m + 1) * P],
                                            sT[:, m, k * P:(k + 1) * P], ident[:, :])
                last.then_inc(d_back, 1)

            def d_step(c, par, first=False, ahead=2):
                if ahead > 0:
                    project(c + 1, 1 - par, first)
                if ahead > 1:
                    turn(c + 2, par)
                turn_back(c, first)

            pe.wait_ge(dve_consts, 1)
            turn(0, 0, True)
            project(0, 0, True)
            turn(1, 1)
            d_step(0, 0, True)
            with pe.Fori(0, 2) as i:
                d_step(2 * i + 1, 1)
                d_step(2 * i + 2, 0)
            d_step(5, 1)
            d_step(6, 0, ahead=1)
            d_step(7, 1, ahead=0)

        @block.scalar
        def _(act):
            st = Steps(act, act_step)
            x_v = t["L0_attn_x"].rearrange("b (h k p) e -> h b p k e", h=2, p=P)

            def deviation(c):
                act.wait_ge(a_stats, c + 1)
                act.activation(rst, mv[:, :, 1], ACT.Sqrt).then_inc(a_sd, 1)

            def copy_turned(c, h):
                act.wait_ge(a_transposed, c + 1)
                if not (isinstance(c, int) and c < 2):
                    act.wait_ge(x_stored, 16 * (c - 1))
                for m in range(KT):
                    act.copy(xst[:, h, m], ps[:, m]).then_inc(a_xt, 1)

            def copy_v(c, h):
                act.wait_ge(a_proj_v, c + 1)
                if not (isinstance(c, int) and c < 2):
                    act.wait_ge(a_v_out, 16 * TB * (c - 1))
                act.copy(vst[:, h].rearrange("p k n -> p (k n)"), ps[:, 6]).then_inc(a_vst, 1)

            def high_part(c, h, tile):
                act.wait_ge(a_roped, 3 * c + tile + 1)
                if tile == 0 and not (isinstance(c, int) and c < 2):
                    act.wait_ge(a_qk_out[h], 96 * (c // 2))
                dst = qhl[:, h, tile] if tile < 2 else khl[:, h]
                act.copy(dst[:, 0], roped[tile]).then_inc(a_high, 1)

            def a_step(c, h, ahead=2):
                if ahead > 1:
                    act.dma_start(xin[:, h], x_v[h, c // 2 + 1]).then_inc(a_xin[h], 16)
                high_part(c, h, 0)
                copy_v(c, h)
                if ahead > 0:
                    copy_turned(c + 1, 1 - h)
                high_part(c, h, 1)
                high_part(c, h, 2)
                if ahead > 1:
                    deviation(c + 2)

            deviation(0)
            copy_turned(0, 0)
            deviation(1)
            act.wait_ge(dve_consts, 1)
            act.activation(lame, lams, ACT.Exp).then_inc(act_consts, 1)
            a_step(0, 0)
            a_step(1, 1)
            with act.Fori(1, B - 1) as b:
                a_step(2 * b, 0)
                a_step(2 * b + 1, 1)
            a_step(NCH - 2, 0, 1)
            a_step(NCH - 1, 1, 0)

            act.wait_ge(a_split, 3 * NCH)
            act.wait_ge(a_v_out, 16 * TB * NCH)
            act.wait_ge(x_stored, 16 * NCH)
            act.wait_ge(a_transposed, NCH)

            def ot_evacuate(u, h):
                act.wait_ge(b_pv, JOBS * u + (16 if h == 0 else JOBS))
                if not (isinstance(u, int) and u == 0 and h == 0):
                    act.wait_ge(b_ot_turned, 2 * u + h)
                act.copy(otsb, ps[:, 6]).then_inc(b_ot_out, 1)

            def unit(u, par, first, last=False):
                for s in range(JOBS):
                    if last and s == FFN_SPLIT_AT:
                        split_x(0, 0, True)
                    if last and s == FFN_EXP_AT:
                        route_exp(0)
                    (h, j), m = GROUPS[s // MAPS], s % MAPS
                    act.wait_ge(b_scores, JOBS * u + s + 1)
                    if m == 0 and not (first and s < PRING):
                        act.wait_ge(b_pv, JOBS * u + s - MAPS)
                    t0 = max(0, P * j - C * h)
                    act.activation(probs[:, s % PRING, t0:C], ps[:, s % SRING, t0:C], ACT.Exp, scale=SCALE
                                   ).then_inc(b_exp, 1)
                    if s == OT_EVAC_B_AT and not first:
                        ot_evacuate(u - 1, 1)
                    if s == OT_EVAC_A_AT:
                        ot_evacuate(u, 0)

            def split_x(cc, par, first):
                act.wait_ge(c_xin[par], 16 * (cc // 2 + 1))
                if not first:
                    act.wait_ge(c_up, 2 * NE * (cc - 1))
                for k in range(KT):
                    act.copy(xh[:, par, k], xc[:, par, k]).then_inc(c_xh, 1)

            def hidden(cc, e, gp, first=False):
                G = NE * cc + e
                for m in range(KT):
                    act.wait_ge(c_up, 2 * G + m + 1)
                    if not first and m == 0:
                        act.wait_ge(c_gate, 2 * G)
                    act.activation(hh[:, m], ps[:, m], ACT.Identity, bias=bup[:, e, m:m + 1])
                    if not first:
                        act.wait_ge(c_u, 2 * (G - 2) + m + 1)
                    act.activation(h32[:, gp, m], ps[:, m], ACT.Identity, bias=bup[:, e, m:m + 1]
                                   ).then_inc(c_h32, 1)

            def split_u(cc, d, par, first):
                e = d if d < NEXP else NE - 1
                D = (NEXP + 1) * cc + d
                for m in range(KT):
                    act.wait_ge(c_u, 2 * (NE * cc + e) + m + 1)
                    if m == 0 and not (first and d < 2):
                        act.wait_ge(c_down, D - 1)
                    act.copy(uh[:, (par + d) % 2, m], su[:, e % 2, m]).then_inc(c_uh, 1)

            def chunk(cc, par, first, last):
                for e in range(NE):
                    G = NE * cc + e
                    for m in range(KT):
                        act.wait_ge(c_gate, 2 * G + m + 1)
                        if e == 0:
                            if not first:
                                act.wait_ge(c_u, 2 * G - 1 + m)
                        elif not (first and e == 1):
                            act.wait_ge(c_ul, 2 * ((NEXP + 1) * cc + e - 1) - 1 + m)
                        act.activation(su[:, e % 2, m], ps[:, 2 + m], ACT.Silu,
                                       bias=bg[:, min(e, NEXP), m:m + 1]).then_inc(c_silu, 1)
                    if e == 1 and not first:
                        square(cc - 1, False)
                    if e < NE - 1:
                        hidden(cc, e + 1, (e + 1) % 2, first=first and e == 0)
                    elif not last:
                        hidden(cc + 1, 0, 0)
                    if e == 5:
                        if not first:
                            inv_rms(cc - 1)
                        if not last:
                            route_exp(cc + 1)
                    elif e == 6:
                        split_u(cc, 5, par, first)
                    else:
                        split_u(cc, min(e, NEXP), par, first)
                    if e == 3 and not last:
                        split_x(cc + 1, 1 - par, first)

            def square(cc, first):
                for m in range(KT):
                    act.wait_ge(c_y, 2 * cc + m + 1)
                    act.activation(sq[:, m], ysb[:, m], ACT.Square).then_inc(c_sq, 1)

            def inv_rms(cc):
                act.wait_ge(c_msread, cc + 1)
                act.activation(rs, rs, ACT.Ln, bias=epsn).then_inc(c_ln, 1)
                act.wait_ge(c_ln, cc + 1)
                act.activation(rs, rs, ACT.Exp, scale=-0.5).then_inc(c_rs, 1)

            def route_exp(cc):
                act.wait_ge(c_lg, cc + 1)
                act.activation(wgt, gg, ACT.Exp).then_inc(c_re, 1)

            unit(0, 0, True)
            with act.Fori(0, UNITS // 2 - 1) as i:
                unit(2 * i + 1, 1, False)
                unit(2 * i + 2, 0, False)
            unit(UNITS - 1, 1, False, True)
            ot_evacuate(UNITS - 1, 1)

            act.wait_ge(ffn_w_ready, FFN_W_STEPS)
            hidden(0, 0, 0, first=True)
            chunk(0, 0, True, False)
            total = LAYERS * NCH
            with act.Fori(0, total // 2 - 1) as i:
                chunk(2 * i + 1, 1, False, False)
                chunk(2 * i + 2, 0, False, False)
            chunk(total - 1, 1, False, True)
            square(total - 1, False)
            inv_rms(total - 1)

            def copy_turned(c, first=False):
                act.wait_ge(d_turned, c + 1)
                if not first:
                    act.wait_ge(d_proj, c)
                for m in range(KT):
                    act.copy(aT[:, m], ps[:, m]).then_inc(d_aT, 1)

            def silu(c, par, first=False):
                act.wait_ge(d_gin[par], 16 * KT * (c // 2 + 1))
                if not first:
                    act.wait_ge(d_s, 2 * c)
                for m in range(KT):
                    act.activation(sgT[:, m], gT[par][m], ACT.Silu).then_inc(d_silu, 1)

            def d_step(c, par, ahead=2):
                if ahead > 1:
                    copy_turned(c + 2)
                if ahead > 0:
                    silu(c + 1, 1 - par)

            copy_turned(0, True)
            copy_turned(1)
            act.wait_ge(c_xnew, 2 * total)
            silu(0, 0, True)
            d_step(0, 0)
            with act.Fori(0, 2) as i:
                d_step(2 * i + 1, 1)
                d_step(2 * i + 2, 0)
            d_step(5, 1)
            d_step(6, 0, ahead=1)

        @block.vector
        def _(dve):
            st = Steps(dve, dve_step)

            def go(ins):
                st.done(ins)
                st.wait()

            def make_consts():
                dve.wait_ge(consts_in, 16 * N_CONSTS)
                st.done(dve.memset(epsn, 1e-6))
                for i in range(2):
                    st.done(dve.tensor_tensor(lamp[:, i], lamv[:, 2 * i], lamv[:, 2 * i + 1], ALU.mult))
                st.done(dve.tensor_scalar(rmsw, rmsw, 1.0 - LAMBDA_INIT, None, ALU.mult))
                st.done(dve.tensor_scalar(bds, bds, float(NSH), None, ALU.mult))
                st.wait()
                st.done(dve.tensor_reduce(lams, lamp, AX, ALU.add))
                st.wait()
                dve.tensor_scalar(wo[:, :, :].rearrange("p k n -> p (k n)"), wo[:, :, :].rearrange("p k n -> p (k n)"),
                                  rmsw, None, ALU.mult).then_inc(dve_consts, 1)
                dve.wait_ge(act_consts, 1)
                go(dve.tensor_tensor(lamneg, lame[:, 1:2], lame[:, 0:1], ALU.subtract))
                go(dve.tensor_scalar(lamneg, lamneg, -LAMBDA_INIT, None, ALU.add))

            def norm_chunk(c, h):
                dve.wait_ge(a_xin[h], 16 * (c // 2 + 1))
                for k in range(TB):
                    st.done(dve.bn_stats(bst[:, k], xin[:, h, k]))
                st.wait()
                st.done(dve.tensor_copy(rst[:, 0:1], bst[:, 0, 0:1]))
                for k in range(TB):
                    st.done(dve.bn_aggr(mv[:, k], bst[:, k]))
                st.wait()
                dve.tensor_scalar(mv[:, :, 1], mv[:, :, 1], 1e-5, None, ALU.add).then_inc(a_stats, 1)
                dve.wait_ge(a_sd, c + 1)
                go(dve.reciprocal(rst, rst))
                for k in range(TB):
                    dve.tensor_scalar(xin[:, h, k], xin[:, h, k], mv[:, k, 0:1], rst[:, k:k + 1],
                                      ALU.subtract, ALU.mult).then_inc(a_normed, 1)

            def rope_chunk(c, h):
                ts = slice(C * h, C * (h + 1))
                cs, sn = cosT[:, ts], sinT[:, ts]
                dve.wait_ge(a_proj_q, c + 1)
                if not (isinstance(c, int) and c < 2):
                    dve.wait_ge(a_qk_out[h], 96 * (c // 2))

                def low_part(tile):
                    dve.wait_ge(a_high, 3 * c + tile + 1)
                    dst = qhl[:, h, tile] if tile < 2 else khl[:, h]
                    dve.tensor_tensor(dst[:, 1], roped[tile], dst[:, 0].bitcast(F32), ALU.subtract
                                      ).then_inc(a_split, 1)

                for tile in range(3):
                    if tile == 2:
                        dve.wait_ge(a_proj_k, c + 1)
                    one, two = ((2, 3), (3, 2), (4, 5))[tile]
                    follows = not (isinstance(c, int) and c == 0)
                    if tile == 2 or (tile == 0 and follows):
                        dve.wait_ge(a_split, 3 * c + tile // 2)
                    st.done(dve.tensor_tensor(roped[tile], ps[:, one], cs, ALU.mult))
                    if tile > 0 or follows:
                        dve.wait_ge(a_roped, 3 * c + tile)
                    if tile < 2:
                        st.done(dve.tensor_tensor(ropeB, ps[:, two], sn, ALU.mult))
                    else:
                        st.done(dve.scalar_tensor_tensor(ropeB, ps[:, two], sgn, sn, ALU.mult, ALU.mult))
                    st.wait()
                    dve.tensor_tensor(roped[tile], roped[tile], ropeB, ALU.subtract if tile == 1 else ALU.add
                                      ).then_inc(a_roped, 1)
                    if tile > 0:
                        low_part(tile - 1)
                low_part(2)

            norm_chunk(0, 0)
            clear_stacks(dve, st, 0)
            norm_chunk(1, 1)
            make_consts()
            for c in range(2):
                rope_chunk(c, c)
                norm_chunk(c + 2, c)
            with dve.Fori(1, B - 1) as b:
                st.enter(b - 1, A_STEPS)
                for h in range(2):
                    rope_chunk(2 * b + h, h)
                    norm_chunk(2 * b + h + 2, h)
                st.leave(B - 2)
            for h in range(2):
                rope_chunk(NCH - 2 + h, h)

            TR = 7

            def reduce_max(u, s):
                i, piece, m = MAXJ[s]
                width = min(512, P * (i + 1) - 512 * piece)
                dve.wait_ge(b_maxs, JOBS * u + s + 1)
                n = 4 * m + i % 4
                dve.tensor_reduce(mx[:, i // 4, piece, n:n + 1], ps[:, SRING + s % SRING, 0:width], AX, ALU.max,
                                  negate=True).then_inc(b_maxed, 1)

            def shift_parts(u, h, par, first):
                dve.wait_ge(b_maxed, JOBS * u + (MAXA if h == 0 else JOBS))
                if h == 1:
                    go(dve.tensor_tensor(mx[:, 1, 0], mx[:, 1, 0], mx[:, 1, 1], ALU.min))
                if not first:
                    dve.wait_ge(b_mturned, 2 * u - 1 + h)
                dve.tensor_copy(mparts[:, h, 0], mx[:, h, 0]).then_inc(b_mparts, 1)
                dve.wait_ge(b_mparts, 2 * (2 * u + h) + 1)
                dve.tensor_tensor(mparts[:, h, 1], mx[:, h, 0], mparts[:, h, 0].bitcast(F32), ALU.subtract
                                  ).then_inc(b_mparts, 1)

            def shift_rows(u, h, par, first):
                dve.wait_ge(b_mturned, 2 * u + h + 1)
                if not first:
                    dve.wait_ge(b_shift_in[1 - par][h], 16 * ((u + 1) // 2))
                dve.tensor_copy(mrows[:, h], ps[0:32, TR, 0:P]).then_inc(b_mrows, 1)

            def combine(u, h, first):
                dve.wait_ge(b_ot_turned, 2 * u + h + 1)
                v = ps[:, TR, :].rearrange("p (n d) -> p n d", d=32)
                go(dve.reciprocal(rec[:, :], v[:, :, VD]))
                r2v = rec[:, :].rearrange("p (n c) -> p n c", c=2)[:, :, 1]
                go(dve.tensor_scalar(r2v, r2v, lamneg, None, ALU.mult))
                dve.tensor_tensor(ot_e, v[:, :, 0:VD], rec[:, :].unsqueeze(2).broadcast_to((P, 16, VD)), ALU.mult
                                  ).then_inc(b_ot_read, 1)
                dve.wait_ge(b_ot_read, 2 * u + h + 1)
                if h == 0 and not first:
                    for half in range(2):
                        dve.wait_ge(b_attn_out[half], 16 * u)
                ev = ot_e.rearrange("p (n c) d -> p n c d", c=2)
                dve.tensor_tensor(attn_st[:, h].rearrange("p k (r d) -> p (k r) d", r=2), ev[:, :, 0], ev[:, :, 1],
                                  ALU.add).then_inc(b_attn, 1)

            def unit(u, par, first, last):
                for s in range(JOBS):
                    w = s + LEAD
                    if w < JOBS:
                        reduce_max(u, w)
                        if w == JOBS - 1:
                            shift_parts(u, 1, par, first)
                    elif not last:
                        w -= JOBS
                        reduce_max(u + 1, w)
                        if w == MAXA - 1:
                            shift_parts(u + 1, 0, 1 - par, False)
                    if s == SHIFT_B_AT:
                        shift_rows(u, 1, par, first)
                    if s == OT_B_AT and not first:
                        combine(u - 1, 1, False)
                    if s == OT_A_AT:
                        combine(u, 0, first)
                    if s == SHIFT_A_AT and not last:
                        shift_rows(u + 1, 0, 1 - par, False)
                    if last and s == FFN_SPLIT_AT:
                        split_x(0, 0)
                    if last and s == SHIFT_A_AT:
                        route_a(0)
                        for part in range(3):
                            route_b(0, 0, part)
                    if last and s == FFN_EXP_AT:
                        route_c(0, 0)

            def split_x(cc, par):
                for k in range(KT):
                    dve.wait_ge(c_xh, KT * cc + k + 1)
                    dve.tensor_tensor(xl[:, par, k], xc[:, par, k], xh[:, par, k].bitcast(F32), ALU.subtract
                                      ).then_inc(c_xl, 1)

            def hidden_low(cc, e):
                G = NE * cc + e
                for m in range(KT):
                    dve.wait_ge(c_h32, 2 * G + m + 1)
                    dve.tensor_tensor(hl[:, m], h32[:, e % 2, m], hh[:, m].bitcast(F32), ALU.subtract
                                      ).then_inc(c_hl, 1)

            def gated(cc, e, m):
                G = NE * cc + e
                dve.wait_ge(c_silu, 2 * G + m + 1)
                s = su[:, e % 2, m]
                if e < NEXP:
                    go(dve.tensor_tensor(s, s, h32[:, e % 2, m], ALU.mult))
                    dve.wait_ge(c_wb, NEXP * cc + e + 1)
                    dve.tensor_tensor(s, s, ps[:, 6], ALU.mult).then_inc(c_u, 1)
                elif e == NEXP:
                    dve.tensor_tensor(s, s, h32[:, e % 2, m], ALU.mult).then_inc(c_u, 1)
                else:
                    go(dve.tensor_tensor(s, s, h32[:, e % 2, m], ALU.mult))
                    dve.tensor_tensor(s, s, su[:, 0, m], ALU.add).then_inc(c_u, 1)

            def u_low(cc, d, par):
                e = d if d < NEXP else NE - 1
                D = (NEXP + 1) * cc + d
                for m in range(KT):
                    dve.wait_ge(c_uh, 2 * D + m + 1)
                    dve.tensor_tensor(ul[:, (par + d) % 2, m], su[:, e % 2, m], uh[:, (par + d) % 2, m].bitcast(F32),
                                      ALU.subtract).then_inc(c_ul, 1)

            def residual(cc, par, first):
                if not first:
                    dve.wait_ge(x_stored, 16 * (NCH + cc))
                dve.wait_ge(c_down, (NEXP + 1) * (cc + 1))
                for m in range(KT):
                    dve.scalar_tensor_tensor(ysb[:, m], ps[:, 4 + m], bds[:, m:m + 1], xc[:, par, m], ALU.add, ALU.add
                                             ).then_inc(c_y, 1)

            def keep_mean_square(cc):
                dve.wait_ge(c_ms, cc + 1)
                dve.tensor_copy(rs, ps[:, 7]).then_inc(c_msread, 1)

            def new_x(cc, layer):
                dve.wait_ge(c_rs, cc + 1)
                for m in range(KT):
                    w = nw[:, layer, m:m + 1] if isinstance(layer, int) else \
                        nw.rearrange("p j k -> p (j k)")[:, bass.ds(layer * KT + m, 1)]
                    dve.scalar_tensor_tensor(ysb[:, m], ysb[:, m], w, rs, ALU.mult, ALU.mult).then_inc(c_xnew, 1)

            def lay(v, layer):
                return v[:, layer] if isinstance(layer, int) else \
                    v.rearrange("p j k -> p (j k)")[:, bass.ds(layer * NEXP, NEXP)]

            def route_a(cc):
                dve.wait_ge(c_logits, cc + 1)
                dve.tensor_copy(lgT, ps[0:32, 7]).then_inc(c_logits_read, 1)

            def route_b(cc, layer, part):
                if part == 0:
                    dve.wait_ge(c_logits_read, cc + 1)
                    go(dve.transpose(lgt.rearrange("p a b -> p (a b)"), lgT))
                    lg = lgt[:, :, 0:NEXP] if isinstance(layer, int) and layer == 0 else \
                        (lgt[:, :, NEXP:2 * NEXP] if isinstance(layer, int)
                         else lgt[:, :, bass.ds(layer * NEXP, NEXP)])
                    go(dve.tensor_tensor(gg, lg, lay(rb, layer).unsqueeze(1).broadcast_to((32, 16, NEXP)), ALU.add))
                    go(dve.tensor_tensor(biased, gg, lay(gb, layer).unsqueeze(1).broadcast_to((32, 16, NEXP)),
                                         ALU.add))
                elif part == 1:
                    go(dve.tensor_tensor(cmp, biased.unsqueeze(2).broadcast_to((32, 16, NEXP, NEXP)),
                                         biased.unsqueeze(3).broadcast_to((32, 16, NEXP, NEXP)), ALU.is_gt))
                    go(dve.tensor_tensor(cmp, cmp, upper.unsqueeze(1).broadcast_to((32, 16, NEXP, NEXP)), ALU.mult))
                    st.done(dve.tensor_reduce(r1, cmp, AX, ALU.add))
                    go(dve.tensor_reduce(r2, cmp.rearrange("p n e j -> p n j e"), AX, ALU.add))
                else:
                    go(dve.tensor_tensor(r1, r1, r2, ALU.subtract))
                    go(dve.tensor_tensor(sel, r1, thr.unsqueeze(1).broadcast_to((32, 16, NEXP)), ALU.is_lt))
                    st.done(dve.tensor_tensor(gg, gg, sel, ALU.mult))
                    go(dve.tensor_scalar(r1, sel, -NEG, NEG, ALU.mult, ALU.add))
                    go(dve.tensor_tensor(gg, gg, r1, ALU.add))
                    go(dve.tensor_reduce(rsum, gg, AX, ALU.max))
                    dve.tensor_tensor(gg, gg, rsum.unsqueeze(2).broadcast_to((32, 16, NEXP)), ALU.subtract
                                      ).then_inc(c_lg, 1)

            def route_c(cc, par):
                dve.wait_ge(c_re, cc + 1)
                go(dve.tensor_reduce(rsum, wgt, AX, ALU.add))
                go(dve.reciprocal(rsum, rsum))
                go(dve.tensor_tensor(wgt, wgt, rsum.unsqueeze(2).broadcast_to((32, 16, NEXP)), ALU.mult))
                go(dve.tensor_copy(whl[:, :, 0:NEXP], wgt))
                go(dve.tensor_tensor(whl[:, :, NEXP:2 * NEXP], wgt, whl[:, :, 0:NEXP].bitcast(F32), ALU.subtract))
                go(dve.transpose(lgT, whl[:, :, :].rearrange("p a b -> p (a b)").bitcast(F32)))
                dve.tensor_copy(wT[:, par], lgT).then_inc(c_wT, 1)

            def chunk(cc, par, first, last, layer_now, layer_next):
                for e in range(NE):
                    gated(cc, e, 0)
                    if e < NE - 1:
                        hidden_low(cc, e + 1)
                    elif not last:
                        hidden_low(cc + 1, 0)
                    gated(cc, e, 1)
                    if e == 6:
                        u_low(cc, 5, par)
                    elif e != 5:
                        u_low(cc, min(e, NEXP), par)
                    if not first:
                        if e == 0:
                            residual(cc - 1, 1 - par, False)
                        if e == 1:
                            keep_mean_square(cc - 1)
                        if e == 6:
                            new_x(cc - 1, layer_now)
                    if not last:
                        if e == 2:
                            route_a(cc + 1)
                        if e in (2, 3, 4):
                            route_b(cc + 1, layer_next, e - 2)
                        if e == 5:
                            split_x(cc + 1, 1 - par)
                        if e == 6:
                            route_c(cc + 1, 1 - par)

            for s in range(LEAD):
                reduce_max(0, s)
                if s == MAXA - 1:
                    shift_parts(0, 0, 0, True)
                if s == MAXA + 4:
                    shift_rows(0, 0, 0, True)
            unit(0, 0, True, False)
            with dve.Fori(0, UNITS // 2 - 1) as i:
                st.enter(i, B_STEPS)
                unit(2 * i + 1, 1, False, False)
                unit(2 * i + 2, 0, False, False)
                st.leave(UNITS // 2 - 1)
            unit(UNITS - 1, 1, False, True)
            combine(UNITS - 1, 1, False)

            dve.wait_ge(b_scores, JOBS * UNITS)
            dve.wait_ge(b_pv, JOBS * UNITS)
            dve.wait_ge(b_ot_turned, 2 * UNITS)
            hidden_low(0, 0)
            total = LAYERS * NCH
            chunk(0, 0, True, False, 0, 0)
            for h in range(2):
                dve.wait_ge(b_attn_out[h], 16 * UNITS)
            with dve.Fori(0, total // 2 - 1) as i:
                st.enter(i, C_STEPS)
                chunk(2 * i + 1, 1, False, False, (2 * i) // NCH, (2 * i + 2) // NCH)
                chunk(2 * i + 2, 0, False, False, (2 * i + 1) // NCH, (2 * i + 3) // NCH)
                st.leave(total // 2 - 1)
            chunk(total - 1, 1, False, True, LAYERS - 1, None)
            residual(total - 1, 1, False)
            keep_mean_square(total - 1)
            new_x(total - 1, LAYERS - 1)

            def gate_s(c, par, first=False):
                dve.wait_ge(d_proj, c + 1)
                if not first:
                    dve.wait_ge(d_back, c)
                for m in range(KT):
                    dve.wait_ge(d_silu, 2 * c + m + 1)
                    dve.tensor_tensor(sT[:, m], ps[:, 2 + 4 * par + m], sgT[:, m], ALU.mult).then_inc(d_s, 1)

            def finish(c, par):
                dve.wait_ge(d_back, c + 1)
                dve.wait_ge(d_xin[par], 16 * (c // 2 + 1))
                xf = xres[:, par].rearrange("p k n -> p (k n)")
                for m in range(2):
                    cols = slice(C * m, C * (m + 1))
                    dve.tensor_tensor(xf[:, cols], xf[:, cols], ps[:, 4 + m], ALU.add).then_inc(d_fin, 1)

            dve.wait_ge(x_stored, 16 * (NCH + total))
            gate_s(0, 0, True)
            finish(0, 0)
            gate_s(1, 1)
            finish(1, 1)
            with dve.Fori(1, NCH // 2) as i:
                for par in range(2):
                    gate_s(2 * i + par, par)
                    finish(2 * i + par, par)


_INS = ["L0_attn_x", "L0_attn_Wq", "L0_attn_Wk", "L0_attn_Wv", "L0_attn_Wo",
        "L0_attn_lambda_q1", "L0_attn_lambda_k1", "L0_attn_lambda_q2", "L0_attn_lambda_k2", "L0_attn_rms_w",
        "L0_ffn_router_W", "L0_ffn_router_b", "L0_ffn_gate_bias", "L0_ffn_exp_Wup", "L0_ffn_exp_bup",
        "L0_ffn_exp_Wg", "L0_ffn_exp_bg", "L0_ffn_exp_Wdown", "L0_ffn_exp_bdown", "L0_ffn_share_Wup",
        "L0_ffn_share_bup", "L0_ffn_share_Wg", "L0_ffn_share_bg", "L0_ffn_share_Wdown", "L0_ffn_share_bdown",
        "L0_ffn_norm_w"]


def shape_constants():
    inv = (1.0 / 10000.0 ** (np.arange(0, HD, 2, dtype=np.float32) / HD)).astype(np.float32)
    freqs = np.outer(np.arange(T, dtype=np.float32), inv).astype(np.float32)
    rows = np.arange(P)
    e = np.arange(NEXP)
    return {
        "rope_cos": np.ascontiguousarray(np.cos(freqs).T[rows // 32]).astype(np.float32),
        "rope_sin": np.ascontiguousarray(np.sin(freqs).T[rows // 32]).astype(np.float32),
        "rope_sign": np.where((rows // 16) % 2 == 0, 1.0, -1.0).astype(np.float32)[:, None],
        "upper": (e[None, :] > e[:, None]).astype(np.float32),
        "thr": (2.0 - e).astype(np.float32),
    }


def kernel(**inputs):
    import concourse.bacc as bacc
    from concourse.bass_utils import run_bass_kernel_spmd

    nc = bacc.Bacc("TRN2", target_bir_lowering=False, num_devices=1)
    arrays, aps = {}, {}
    for name, a in [(n, inputs[n]) for n in _INS] + list(shape_constants().items()):
        a = np.ascontiguousarray(a)
        arrays["in_" + name] = a
        aps[name] = nc.dram_tensor("in_" + name, a.shape, mybir.dt.from_np(a.dtype), kind="ExternalInput").ap()
    out = nc.dram_tensor("out_x", (B, T, E), F32, kind="ExternalOutput").ap()
    build(nc, aps, out)
    r = run_bass_kernel_spmd(nc, [arrays], core_ids=[0])
    return r.results[0]["out_x"]
```
